# Optimizing a Trainium2 kernel written in Bass

```python
import numpy as np
import jax
import jax.numpy as jnp

def _softmax(x, axis=-1):
    return jax.nn.softmax(x, axis=axis)

def _gelu(x):
    return jax.nn.gelu(x, approximate=True)

def _silu(x):
    return jax.nn.silu(x)

def _sigmoid(x):
    return jax.nn.sigmoid(x)

def _layernorm(x, axis=-1, eps=1e-05):
    m = jnp.mean(x, axis=axis, keepdims=True)
    v = jnp.var(x, axis=axis, keepdims=True)
    return (x - m) / jnp.sqrt(v + eps)

def _scatter_add(tgt, idx, src, axis=0):
    return tgt.at[idx].add(src)

def _segment_sum(src, seg, n):
    return jax.ops.segment_sum(src, seg, n)
kernel_name = 'mk_xattn_seq_d1_seqx_r2_03d48e'

def setup_inputs(seed: int=0):
    np.random.seed(seed)
    _w = jnp.asarray

    def _rec_inputs():
        import jax
        import jax.numpy as jnp
        _rk = jax.random.key(seed)
        x = 7.22e-05 + 1 * jax.random.normal(jax.random.fold_in(_rk, 1), (4, 1024, 1024), jnp.float32)
        _lenS = 1024 - jax.random.randint(jax.random.fold_in(_rk, 7), (4,), 0, max(1, 1024 // 4) + 1, jnp.int32)
        _lenS2 = 1601 - jax.random.randint(jax.random.fold_in(_rk, 8), (4,), 0, max(1, 1601 // 4) + 1, jnp.int32)
        _ctx_2048P = jax.random.normal(jax.random.fold_in(_rk, 11), (4, 16, 1024), jnp.float32)
        _ctx_2048c = jax.random.dirichlet(jax.random.fold_in(_rk, 511), 0.3 * jnp.ones((16,), jnp.float32), (4, 1601))
        _ctx_2048t = jnp.einsum('bsk,bkd->bsd', _ctx_2048c, _ctx_2048P)
        _ctx_2048t = _ctx_2048t * jax.lax.rsqrt(jnp.mean(jnp.square(_ctx_2048t)) + 1e-12) * 0.953939
        ctx_2048 = 4.13588e-05 + 0.999923 * (_ctx_2048t + 0.3 * jax.random.normal(jax.random.fold_in(_rk, 611), (4, 1601, 1024), jnp.float32))
        _validS = jnp.arange(1024)[None, :] < _lenS[:, None]
        _validS2 = jnp.arange(1601)[None, :] < _lenS2[:, None]
        _causal = jnp.tril(jnp.ones((1024, 1024), dtype=bool))
        mask_Bx1xSxS2_ff0 = jnp.where(jnp.ones((4, 1, 1024, 1601), dtype=bool), 0.0, -1000000000.0).astype(jnp.float32)
        return (x, ctx_2048, mask_Bx1xSxS2_ff0)
    x, ctx_2048, mask_Bx1xSxS2_ff0 = _rec_inputs()

    def _L0_xattn_setup():
        import jax, jax.numpy as jnp
        import numpy as np
        H = 1024
        NH = 32
        KVH = 8
        HD = H // NH
        GROUPS = NH // KVH
        EPS = 1e-06
        B, L, S = (4, 512, 512)

        def _gqa_forward(hidden_state, encoder_hidden_state, encoder_attention_mask, Wq, bq, Wk, bk, Wv, bv, Wo, bo, gamma, beta):
            b, l, _ = hidden_state.shape
            s = encoder_hidden_state.shape[1]
            q = hidden_state @ Wq + bq
            k = encoder_hidden_state @ Wk + bk
            v = encoder_hidden_state @ Wv + bv
            q = q.reshape(b, l, KVH, GROUPS, HD).transpose(0, 2, 3, 1, 4)
            k = k.reshape(b, s, KVH, HD).transpose(0, 2, 1, 3)
            v = v.reshape(b, s, KVH, HD).transpose(0, 2, 1, 3)
            scale = 1.0 / jnp.sqrt(jnp.asarray(HD, q.dtype))
            scores = jnp.einsum('bkgld,bksd->bkgls', q, k) * scale
            scores = scores + encoder_attention_mask[:, :, None, :, :]
            attn = jax.nn.softmax(scores, axis=-1)
            out = jnp.einsum('bkgls,bksd->bkgld', attn, v)
            out = out.transpose(0, 3, 1, 2, 4).reshape(b, l, H)
            out = out @ Wo + bo
            x = out + hidden_state
            mu = jnp.mean(x, axis=-1, keepdims=True)
            var = jnp.var(x, axis=-1, keepdims=True)
            return (x - mu) * jax.lax.rsqrt(var + EPS) * gamma + beta
        key = jax.random.key(seed)
        ks = jax.random.split(key, 12)
        sd = 0.02
        return {'hidden_state': jax.random.normal(ks[0], (B, L, H), jnp.float32), 'encoder_hidden_state': jax.random.normal(ks[1], (B, S, H), jnp.float32), 'encoder_attention_mask': jnp.zeros((B, 1, L, S), jnp.float32), 'Wq': jax.random.normal(ks[2], (H, H), jnp.float32) * sd, 'bq': jnp.zeros((H,), jnp.float32), 'Wk': jax.random.normal(ks[3], (H, KVH * HD), jnp.float32) * sd, 'bk': jnp.zeros((KVH * HD,), jnp.float32), 'Wv': jax.random.normal(ks[4], (H, KVH * HD), jnp.float32) * sd, 'bv': jnp.zeros((KVH * HD,), jnp.float32), 'Wo': jax.random.normal(ks[5], (H, H), jnp.float32) * sd, 'bo': jnp.zeros((H,), jnp.float32), 'gamma': jnp.ones((H,), jnp.float32), 'beta': jnp.zeros((H,), jnp.float32)}
    _L0_xattn_all = _L0_xattn_setup()
    _L0_xattn_in = {k: v for k, v in _L0_xattn_all.items() if k in ('Wq', 'bq', 'Wk', 'bk', 'Wv', 'bv', 'Wo', 'bo', 'gamma', 'beta')}
    del _L0_xattn_all
    return {'x': x, 'ctx_2048': ctx_2048, 'mask_Bx1xSxS2_ff0': mask_Bx1xSxS2_ff0, 'L0_xattn_Wq': _L0_xattn_in['Wq'], 'L0_xattn_bq': _L0_xattn_in['bq'], 'L0_xattn_Wk': _L0_xattn_in['Wk'], 'L0_xattn_bk': _L0_xattn_in['bk'], 'L0_xattn_Wv': _L0_xattn_in['Wv'], 'L0_xattn_bv': _L0_xattn_in['bv'], 'L0_xattn_Wo': _L0_xattn_in['Wo'], 'L0_xattn_bo': _L0_xattn_in['bo'], 'L0_xattn_gamma': _L0_xattn_in['gamma'], 'L0_xattn_beta': _L0_xattn_in['beta']}

def reference(x, ctx_2048, mask_Bx1xSxS2_ff0, L0_xattn_Wq, L0_xattn_bq, L0_xattn_Wk, L0_xattn_bk, L0_xattn_Wv, L0_xattn_bv, L0_xattn_Wo, L0_xattn_bo, L0_xattn_gamma, L0_xattn_beta):
    import jax
    import jax.numpy as jnp

    def _L0_xattn_ref(hidden_state, encoder_hidden_state, encoder_attention_mask, Wq, bq, Wk, bk, Wv, bv, Wo, bo, gamma, beta):
        import jax, jax.numpy as jnp
        import numpy as np
        H = 1024
        NH = 32
        KVH = 8
        HD = H // NH
        GROUPS = NH // KVH
        EPS = 1e-06
        B, L, S = (4, 512, 512)

        def _gqa_forward(hidden_state, encoder_hidden_state, encoder_attention_mask, Wq, bq, Wk, bk, Wv, bv, Wo, bo, gamma, beta):
            b, l, _ = hidden_state.shape
            s = encoder_hidden_state.shape[1]
            q = hidden_state @ Wq + bq
            k = encoder_hidden_state @ Wk + bk
            v = encoder_hidden_state @ Wv + bv
            q = q.reshape(b, l, KVH, GROUPS, HD).transpose(0, 2, 3, 1, 4)
            k = k.reshape(b, s, KVH, HD).transpose(0, 2, 1, 3)
            v = v.reshape(b, s, KVH, HD).transpose(0, 2, 1, 3)
            scale = 1.0 / jnp.sqrt(jnp.asarray(HD, q.dtype))
            scores = jnp.einsum('bkgld,bksd->bkgls', q, k) * scale
            scores = scores + encoder_attention_mask[:, :, None, :, :]
            attn = jax.nn.softmax(scores, axis=-1)
            out = jnp.einsum('bkgls,bksd->bkgld', attn, v)
            out = out.transpose(0, 3, 1, 2, 4).reshape(b, l, H)
            out = out @ Wo + bo
            x = out + hidden_state
            mu = jnp.mean(x, axis=-1, keepdims=True)
            var = jnp.var(x, axis=-1, keepdims=True)
            return (x - mu) * jax.lax.rsqrt(var + EPS) * gamma + beta
        return _gqa_forward(hidden_state, encoder_hidden_state, encoder_attention_mask, Wq, bq, Wk, bk, Wv, bv, Wo, bo, gamma, beta)
    x = _L0_xattn_ref(x, ctx_2048, mask_Bx1xSxS2_ff0, L0_xattn_Wq, L0_xattn_bq, L0_xattn_Wk, L0_xattn_bk, L0_xattn_Wv, L0_xattn_bv, L0_xattn_Wo, L0_xattn_bo, L0_xattn_gamma, L0_xattn_beta)
    return x

_drawn_inputs = setup_inputs


def setup_inputs(seed=0):
    import zlib

    import numpy as np

    out = dict(_drawn_inputs(seed))
    spreads = {'L0_xattn_bq': (0.0, 0.8),
     'L0_xattn_bk': (0.0, 2.0),
     'L0_xattn_bv': (0.0, 0.1),
     'L0_xattn_bo': (0.0, 0.1),
     'L0_xattn_gamma': (1.0, 0.2),
     'L0_xattn_beta': (0.0, 0.1)}
    factors = {}
    for name, (base, spread) in spreads.items():
        noise = np.random.default_rng([zlib.crc32(name.encode()), seed]).standard_normal(out[name].shape)
        drawn = base * np.exp(spread * noise) if base else spread * noise
        out[name] = jnp.asarray(drawn.astype(out[name].dtype))
    for name, factor in factors.items():
        out[name] = (out[name] * factor).astype(out[name].dtype)
    return out
```

```python
from contextlib import ExitStack

import numpy as np

import concourse.bass as bass
from concourse import mybir

F32 = mybir.dt.float32
F32R = mybir.dt.float32r
ALU = mybir.AluOpType
ACT = mybir.ActivationFunctionType

P = 128
B, L, H = 4, 1024, 1024
S = 1601
NH, KVH, HD = 32, 8, 32
G = NH // KVH
KV = KVH * HD
KT = H // P
SCALE = float(HD) ** -0.5
EPS = 1e-6

XC = 512
NXC = B * L // XC
CC = 402
CSTART = (0, 400, 800, S - CC)
NCC = len(CSTART)
VSUB = (0, 128, 256, CC - P)
LQ = 256
NLQ = B * L // LQ
NSTEP = NLQ * KVH
ROWS = G * LQ // P
ST = -(-S // P)
SLAST = S - (ST - 1) * P
STACK = 3 * HD
FMAX = 3.0e38


SPAD = 1604
HALVES = ((0, 400, 400), (800, 1202, 402))


def xattn_program(nc, x, ctx_kv, mask, wq, bq, wk, bk, wv, bv, wo, bo, gamma, beta, out):
    x_flat = x.rearrange("b l h -> (b l) h")
    ctx_flat = ctx_kv.rearrange("b s h -> (b s) h")
    mask_flat = mask.rearrange("b o l s -> (b o l) s")
    out_flat = out.rearrange("b l h -> (b l) h")

    q_dram = nc.dram_tensor("q_parts", [NLQ, KVH, 2, P, LQ], F32, kind="Internal").ap()
    k_dram = nc.dram_tensor("k_parts", [B, 2, KV, S], F32, kind="Internal").ap()
    v_dram = nc.dram_tensor("v_rows", [B * S, KV], F32, kind="Internal").ap()
    a_dram = nc.dram_tensor("attended", [NSTEP, P, LQ], F32, kind="Internal").ap()

    with ExitStack() as whole:
        ident = whole.enter_context(nc.sbuf_tensor("ident", [P, P], F32))
        project(nc, x_flat, ctx_flat, wq, bq, wk, bk, wv, bv, q_dram, k_dram, v_dram, ident)
        attend(nc, mask_flat, q_dram, k_dram, v_dram, a_dram, ident)
        output(nc, x_flat, wo, bo, gamma, beta, a_dram, out_flat)


def project(nc, x_flat, ctx_flat, wq, bq, wk, bk, wv, bv, q_dram, k_dram, v_dram, ident):
    with ExitStack() as held:
        def sb(name, shape, dt=F32):
            return held.enter_context(nc.sbuf_tensor(name, shape, dt))

        def sem(name):
            return held.enter_context(nc.semaphore(name))

        wq_hi, wq_lo = sb("wq_hi", [P, KT, H], F32R), sb("wq_lo", [P, KT, H], F32R)
        wk_hi, wk_lo = sb("wk_hi", [P, KT, KV], F32R), sb("wk_lo", [P, KT, KV], F32R)
        wv_hi, wv_lo = sb("wv_hi", [P, KT, KV], F32R), sb("wv_lo", [P, KT, KV], F32R)
        bq_col, bk_col = sb("bq_col", [P, KT]), sb("bk_col", [P, KV // P])
        bq_scaled = sb("bq_scaled", [P, KT])
        bv_row = sb("bv_row", [P, KV])

        with ExitStack() as staging:
            w_raw = staging.enter_context(nc.sbuf_tensor("w_raw", [P, KT, H], F32))
            kv_raw = staging.enter_context(nc.sbuf_tensor("kv_raw", [P, 2, KT, KV], F32))
            wq_in, wk_in, wv_in, bias_in = (staging.enter_context(nc.semaphore(n)) for n in ("wq_in", "wk_in", "wv_in", "bias_in"))
            w_hi_done, w_lo_done = (staging.enter_context(nc.semaphore(n)) for n in ("w_hi_done", "w_lo_done"))
            ident_zero, ident_done = (staging.enter_context(nc.semaphore(n)) for n in ("ident_zero", "ident_done"))
            parts = (
                (wq_in, w_raw[:], wq_hi, wq_lo),
                (wk_in, kv_raw[:, 0], wk_hi, wk_lo),
                (wv_in, kv_raw[:, 1], wv_hi, wv_lo),
            )
            block = staging.enter_context(nc.Block())

            @block.sync
            def _(sp):
                sp.dma_start(w_raw[:], wq.rearrange("(t p) n -> p t n", p=P)).then_inc(wq_in, 16)
                sp.dma_start(kv_raw[:, 0], wk.rearrange("(t p) n -> p t n", p=P)).then_inc(wk_in, 16)
                sp.dma_start(kv_raw[:, 1], wv.rearrange("(t p) n -> p t n", p=P)).then_inc(wv_in, 16)
                with nc.allow_non_contiguous_dma(reason="biases by column"):
                    sp.dma_start(bq_col[:], bq.rearrange("(c p) -> p c", p=P)).then_inc(bias_in, 16)
                    sp.dma_start(bk_col[:], bk.rearrange("(c p) -> p c", p=P)).then_inc(bias_in, 16)
                sp.dma_start(bv_row[:], bv.partition_broadcast(P)).then_inc(bias_in, 16)

            @block.scalar
            def _(act):
                for raw_in, raw, hi, _ in parts:
                    act.wait_ge(raw_in, 16)
                    for t in range(KT):
                        nc.scalar.copy(hi[:, t, :], raw[:, t, :]).then_inc(w_hi_done, 1)

            @block.vector
            def _(dve):
                n = 0
                for _, raw, hi, lo in parts:
                    for t in range(KT):
                        n += 1
                        dve.wait_ge(w_hi_done, n)
                        nc.vector.tensor_tensor(lo[:, t, :], raw[:, t, :], hi[:, t, :].bitcast(F32), ALU.subtract).then_inc(w_lo_done, 1)
                dve.wait_ge(bias_in, 48)
                nc.vector.tensor_scalar(bq_scaled[:], bq_col[:], -SCALE, None, ALU.mult).then_inc(w_lo_done, 1)
                dve.wait_ge(w_lo_done, 3 * KT + 1)

            @block.gpsimd
            def _(pool):
                nc.gpsimd.memset(ident[:], 0.0).then_inc(ident_zero, 1)
                pool.wait_ge(ident_zero, 1)
                nc.gpsimd.affine_select(out=ident[:], in_=ident[:], compare_op=ALU.not_equal, fill=1.0, base=0,
                                        pattern=[[-1, P]], channel_multiplier=1).then_inc(ident_done, 1)
                pool.wait_ge(ident_done, 1)

        rows = sb("rows", [P, XC // P, H])
        t_hi = [sb(f"t_hi{i}", [P, KT, XC], F32R) for i in range(2)]
        t_lo = [sb(f"t_lo{i}", [P, KT, XC], F32R) for i in range(2)]
        full = [sb(f"full{i}", [P, XC]) for i in range(2)]
        o_hi = [sb(f"o_hi{i}", [P, XC], F32R) for i in range(2)]
        o_lo = [sb(f"o_lo{i}", [P, XC], F32R) for i in range(2)]
        v_out = [sb(f"v_out{i}", [P, KV]) for i in range(2)]
        turned = [held.enter_context(nc.psum_tensor(f"turned{i}", [P, XC], F32)) for i in range(2)]
        summed = [held.enter_context(nc.psum_tensor(f"summed{i}", [P, XC], F32)) for i in range(4)]

        rows_in = sem("rows_in")
        turn_done = sem("turn_done")
        hi_done = sem("hi_done")
        lo_done = sem("lo_done")
        sum_done = sem("sum_done")
        sum_read = sem("sum_read")
        part_hi = sem("part_hi")
        part_lo = sem("part_lo")
        part_stored = sem("part_stored")
        v_stored = sem("v_stored")
        part_free = [sem(f"part_free{i}") for i in range(2)]
        v_free = [sem(f"v_free{i}") for i in range(2)]

        XG, CG = KT, KV // P + len(VSUB)
        NX_SLICE, NX_SUM, NX_PART = NXC * KT, NXC * XG, NXC * XG // 2

        def slices(kind, c):
            return c * KT if kind == "x" else c * KT + NX_SLICE

        def sums(kind, c):
            return c * XG if kind == "x" else c * CG + NX_SUM

        def landed(kind, c):
            return c * 16 + 16 if kind == "x" else c * 32 + (16 * NXC + 32)

        def width(kind):
            return XC if kind == "x" else CC

        block = held.enter_context(nc.Block())

        @block.sync
        def _(sp):
            def load_x(c):
                sp.dma_start(rows[:], x_flat[bass.ds(c * XC, XC), :].rearrange("(t p) h -> p t h", p=P)).then_inc(rows_in, 16)

            load_x(0)
            with sp.Fori(1, NXC) as c:
                sp.wait_ge(turn_done, c * KT)
                load_x(c)
            with sp.Fori(0, B) as b:
                for n, start in enumerate(CSTART):
                    sp.wait_ge(turn_done, b * (NCC * KT) + (NX_SLICE + n * KT))
                    sp.dma_start(rows[:, 0:3, :], ctx_flat[bass.ds(b * S + start, 3 * P), :].rearrange("(t p) h -> p t h", p=P)).then_inc(rows_in, 16)
                    sp.dma_start(rows[0:CC - 3 * P, 3, :], ctx_flat[bass.ds(b * S + (start + 3 * P), CC - 3 * P), :]).then_inc(rows_in, 16)

        @block.tensor
        def _(pe):
            pe.sem_inc(sum_done, 2 * XG)

            def turn(kind, c):
                n0 = slices(kind, c)
                pe.wait_ge(rows_in, landed(kind, c))
                for t in range(KT):
                    pe.wait_ge(lo_done, n0 + (t + 1))
                    for at in range(0, width(kind), P):
                        w = min(P, width(kind) - at)
                        last = nc.tensor.transpose(turned[t % 2][:, at:at + w], rows[0:w, at // P, t * P:(t + 1) * P], ident[0:w, 0:w])
                    last.then_inc(turn_done, 1)

            def three(acc, pairs):
                n = 0
                for lhs, rhs in pairs:
                    last = nc.tensor.matmul(acc, lhs, rhs, start=(n == 0), stop=(n == len(pairs) - 1))
                    n += 1
                last.then_inc(sum_done, 1)

            def multiply(kind, c, par):
                n0, g = sums(kind, c), 0
                off = 0 if kind == "x" else par * CG
                pe.wait_ge(lo_done, slices(kind, c) + (KT + 2))
                hi, lo = t_hi[par], t_lo[par]
                w_hi, w_lo, tiles = (wq_hi, wq_lo, KT) if kind == "x" else (wk_hi, wk_lo, KV // P)
                for ct in range(tiles):
                    pe.wait_ge(sum_read, n0 + (g + 1))
                    cols = slice(ct * P, (ct + 1) * P)
                    three(summed[(off + g) % 4][:, 0:width(kind)],
                          [(w[:, t, cols], m[:, t, 0:width(kind)]) for w, m in ((w_hi, hi), (w_hi, lo), (w_lo, hi)) for t in range(KT)])
                    g += 1
                if kind == "ctx":
                    for v0 in VSUB:
                        pe.wait_ge(sum_read, n0 + (g + 1))
                        three(summed[(off + g) % 4][:, 0:KV],
                              [(m[:, t, v0:v0 + P], w[:, t, :]) for m, w in ((hi, wv_hi), (lo, wv_hi), (hi, wv_lo)) for t in range(KT)])
                        g += 1

            turn("x", 0)
            with pe.Fori(0, NXC // 2 - 1) as i:
                for par in range(2):
                    turn("x", i * 2 + (par + 1))
                    multiply("x", i * 2 + par, par)
            turn("x", NXC - 1)
            multiply("x", NXC - 2, 0)
            turn("ctx", 0)
            multiply("x", NXC - 1, 1)
            with pe.Fori(0, B * NCC // 2 - 1) as i:
                for par in range(2):
                    turn("ctx", i * 2 + (par + 1))
                    multiply("ctx", i * 2 + par, par)
            turn("ctx", B * NCC - 1)
            multiply("ctx", B * NCC - 2, 0)
            multiply("ctx", B * NCC - 1, 1)

        @block.scalar
        def _(act):
            def split_hi(kind, c, par):
                n0 = slices(kind, c)
                before = c * XG + XG if kind == "x" else (c + 9) * XG if isinstance(c, int) and c < 2 else c * CG + (NX_SUM + 2 * XG - CG)
                act.wait_ge(sum_done, before)
                for t in range(KT):
                    act.wait_ge(turn_done, n0 + (t + 1))
                    nc.scalar.copy(t_hi[par][:, t, 0:width(kind)], turned[t % 2][:, 0:width(kind)]).then_inc(hi_done, 1)

            def parts_hi(kind, c, par):
                n0 = sums(kind, c) + 2 * XG
                off = 0 if kind == "x" else par * CG
                for g in range(KT if kind == "x" else KV // P):
                    act.wait_ge(sum_done, n0 + (g + 1))
                    seq = c * (XG // 2) + g // 2 if kind == "x" else c + NX_PART
                    act.wait_ge(part_free[g % 2], seq + 1)
                    acc = summed[(off + g) % 4][:, 0:width(kind)]
                    if kind == "x":
                        ins = nc.scalar.activation(o_hi[g % 2][:, 0:XC], acc, ACT.Identity, bias=bq_scaled[:, g:g + 1], scale=-SCALE)
                    else:
                        ins = nc.scalar.activation(o_hi[g % 2][:, 0:CC], acc, ACT.Identity, bias=bk_col[:, g:g + 1])
                    ins.then_inc(part_hi, 1)

            split_hi("x", 0, 0)
            with act.Fori(0, NXC // 2 - 1) as i:
                for par in range(2):
                    split_hi("x", i * 2 + (par + 1), 1 - par)
                    parts_hi("x", i * 2 + par, par)
            split_hi("x", NXC - 1, 1)
            parts_hi("x", NXC - 2, 0)
            split_hi("ctx", 0, 0)
            parts_hi("x", NXC - 1, 1)
            split_hi("ctx", 1, 1)
            parts_hi("ctx", 0, 0)
            with act.Fori(0, B * NCC // 2 - 1) as i:
                split_hi("ctx", i * 2 + 2, 0)
                parts_hi("ctx", i * 2 + 1, 1)
                split_hi("ctx", i * 2 + 3, 1)
                parts_hi("ctx", i * 2 + 2, 0)
            parts_hi("ctx", B * NCC - 1, 1)

        @block.vector
        def _(dve):
            dve.sem_inc(lo_done, 2)
            dve.sem_inc(sum_read, 4)

            def split_lo(kind, c, par):
                n0 = slices(kind, c)
                for t in range(KT):
                    dve.wait_ge(hi_done, n0 + (t + 1))
                    w = width(kind)
                    nc.vector.tensor_tensor(t_lo[par][:, t, 0:w], turned[t % 2][:, 0:w], t_hi[par][:, t, 0:w].bitcast(F32), ALU.subtract).then_inc(lo_done, 1)

            def parts_lo(kind, c, par):
                n0 = sums(kind, c)
                p0 = c * XG if kind == "x" else c * (KV // P) + NXC * XG
                off = 0 if kind == "x" else par * CG
                w, tiles = (XC, KT) if kind == "x" else (CC, KV // P)
                for g in range(tiles):
                    dve.wait_ge(part_hi, p0 + (g + 1))
                    acc = summed[(off + g) % 4][:, 0:w]
                    if kind == "x":
                        ins = nc.vector.tensor_scalar(full[g % 2][:, 0:w], acc, -SCALE, bq_scaled[:, g:g + 1], ALU.mult, ALU.add)
                    else:
                        ins = nc.vector.tensor_scalar(full[g % 2][:, 0:w], acc, bk_col[:, g:g + 1], None, ALU.add)
                    ins.then_inc(sum_read, 1)
                    dve.wait_ge(sum_read, n0 + (g + 5))
                    nc.vector.tensor_tensor(o_lo[g % 2][:, 0:w], full[g % 2][:, 0:w], o_hi[g % 2][:, 0:w].bitcast(F32), ALU.subtract).then_inc(part_lo, 1)
                if kind == "ctx":
                    for j in range(len(VSUB)):
                        g = tiles + j
                        dve.wait_ge(sum_done, n0 + (g + 1 + 2 * XG))
                        dve.wait_ge(v_free[j % 2], c * 2 + (j // 2 + 1))
                        nc.vector.tensor_tensor(v_out[j % 2][:], summed[(off + g) % 4][:, 0:KV], bv_row[:], ALU.add).then_inc(sum_read, 1)

            split_lo("x", 0, 0)
            with dve.Fori(0, NXC // 2 - 1) as i:
                for par in range(2):
                    split_lo("x", i * 2 + (par + 1), 1 - par)
                    parts_lo("x", i * 2 + par, par)
            split_lo("x", NXC - 1, 1)
            parts_lo("x", NXC - 2, 0)
            split_lo("ctx", 0, 0)
            parts_lo("x", NXC - 1, 1)
            with dve.Fori(0, B * NCC // 2 - 1) as i:
                for par in range(2):
                    split_lo("ctx", i * 2 + (par + 1), 1 - par)
                    parts_lo("ctx", i * 2 + par, par)
            split_lo("ctx", B * NCC - 1, 1)
            parts_lo("ctx", B * NCC - 2, 0)
            parts_lo("ctx", B * NCC - 1, 1)

        @block.gpsimd
        def _(pool):
            for i in range(2):
                pool.sem_inc(part_free[i], 1)
                pool.sem_inc(v_free[i], 1)
            with pool.Fori(0, NXC) as c:
                for g in range(KT):
                    pool.wait_ge(part_lo, c * XG + (g + 1))
                    for n, part in enumerate((o_hi, o_lo)):
                        dst = q_dram[bass.ds(c * (XC // LQ), XC // LQ), g, n].rearrange("a p l -> p a l")
                        pool.dma_start(dst, part[g % 2][:, 0:XC].bitcast(F32).rearrange("p (a l) -> p a l", l=LQ)).then_inc(part_stored, 16)
                    pool.wait_ge(part_stored, c * (32 * XG) + 32 * (g + 1))
                    pool.sem_inc(part_free[g % 2], 1)
            with pool.Fori(0, B) as b:
                for n, start in enumerate(CSTART):
                    for g in range(KV // P):
                        seq = NXC * XG + n * (KV // P) + g + 1
                        pool.wait_ge(part_lo, b * (NCC * KV // P) + seq)
                        for m, part in enumerate((o_hi, o_lo)):
                            dst = k_dram[bass.ds(b, 1), m, g * P:(g + 1) * P, start:start + CC].rearrange("b p s -> (b p) s")
                            pool.dma_start(dst, part[g % 2][:, 0:CC].bitcast(F32)).then_inc(part_stored, 16)
                        pool.wait_ge(part_stored, b * (32 * NCC * KV // P) + 32 * seq)
                        pool.sem_inc(part_free[g % 2], 1)
                    for j, v0 in enumerate(VSUB):
                        pool.wait_ge(sum_read, b * (NCC * CG) + (NX_SUM + n * CG + KV // P + j + 1 + 4))
                        pool.dma_start(v_dram[bass.ds(b * S + (start + v0), P), :], v_out[j % 2][:]).then_inc(v_stored, 16)
                        pool.wait_ge(v_stored, b * (16 * NCC * len(VSUB)) + 16 * (n * len(VSUB) + j + 1))
                        pool.sem_inc(v_free[j % 2], 1)


def attend(nc, mask_flat, q_dram, k_dram, v_dram, a_dram, ident):
    PAIRS = NSTEP // 2
    RP = 2 * ROWS
    AHEAD = 3
    GROUPS = ((0, 4), (4, 8), (8, 12), (12, 13))
    with ExitStack() as held:
        def sb(name, shape, dt=F32):
            return held.enter_context(nc.sbuf_tensor(name, shape, dt))

        def sem(name):
            return held.enter_context(nc.semaphore(name))

        q_sb = [sb(f"q_sb{i}", [STACK, G, LQ], F32R) for i in range(2)]
        k_sb = [sb(f"k_sb{i}", [STACK, SPAD], F32R) for i in range(2)]
        v_sb = [sb(f"v_sb{i}", [P, ST, HD]) for i in range(2)]
        mask_raw = sb("mask_raw", [P, LQ // P, S])
        neg_mask = sb("neg_mask", [P, LQ // P, SPAD])
        weights = [sb(f"weights{i}", [P, SPAD]) for i in range(4)]
        row_min = sb("row_min", [P, 4, 2])
        denom = [sb(f"denom{i}", [P, ROWS]) for i in range(2)]
        recip_col = sb("recip_col", [P, ROWS])
        recip = sb("recip", [P, ROWS, HD])
        w_t = [sb(f"w_t{i}", [P, ST, G, LQ]) for i in range(2)]
        recip_t = sb("recip_t", [P, LQ])
        attended = [sb(f"attended{i}", [P, LQ]) for i in range(2)]
        score = [held.enter_context(nc.psum_tensor(f"score{i}", [P, 2, 512], F32)) for i in range(2)]
        turned = [held.enter_context(nc.psum_tensor(f"w_turned{i}", [P, 4, P], F32)) for i in range(3)]
        mixed = held.enter_context(nc.psum_tensor("mixed", [P, 2, LQ], F32))

        pad_done = sem("pad_done")
        mask_in = [sem(f"mask_in{i}") for i in range(2)]
        mask_free = [sem(f"mask_free{i}") for i in range(2)]
        mask_ready = [sem(f"mask_ready{i}") for i in range(2)]
        qk_in = [sem(f"qk_in{i}") for i in range(2)]
        v_in = [sem(f"v_in{i}") for i in range(2)]
        qk_done = sem("qk_done")
        min_done = sem("min_done")
        half_seen = sem("half_seen")
        exp_done = sem("exp_done")
        turn_done = sem("w_turn_done")
        copied_dve = sem("copied_dve")
        copied_act = sem("copied_act")
        recip_done = sem("recip_done")
        recip_seen = sem("recip_seen")
        wide_done = sem("wide_done")
        mix_done = sem("mix_done")
        recip_t_done = sem("recip_t_done")
        norm_done = sem("norm_done")
        stored = [sem(f"stored{i}") for i in range(2)]

        block = held.enter_context(nc.Block())

        @block.sync
        def _(sp):
            with sp.Fori(0, B) as b:
                with sp.Fori(0, L // LQ) as lq:
                    for lt in range(LQ // P):
                        sp.wait_ge(mask_free[lt], b * (L // LQ) + lq + 1)
                        sp.dma_start(mask_raw[:, lt, :], mask_flat[bass.ds(b * L + lq * LQ + lt * P, P), :]).then_inc(mask_in[lt], 16)
                    with sp.Fori(0, KVH // 2) as kp:
                        for j in range(2):
                            step = b * (L // LQ * KVH) + lq * KVH + kp * 2 + j
                            sp.wait_ge(qk_done, step * (2 * ROWS) + 2 * ROWS)
                            for r, part in enumerate((0, 1, 0)):
                                src = q_dram[bass.ds(b * (L // LQ) + lq, 1), bass.ds(kp * 2 + j, 1), part].rearrange("a k (h d) l -> (a k d) h l", d=HD)
                                sp.dma_start(q_sb[j][r * HD:(r + 1) * HD].bitcast(F32), src).then_inc(qk_in[j], 16)
                            for r, part in enumerate((0, 0, 1)):
                                src = k_dram[bass.ds(b, 1), part, bass.ds(kp * (2 * HD) + j * HD, HD), :].rearrange("b d s -> (b d) s")
                                sp.dma_start(k_sb[j][r * HD:(r + 1) * HD, 0:S].bitcast(F32), src).then_inc(qk_in[j], 16)
                            sp.wait_ge(mix_done, step + 1)
                            cols = bass.ds(kp * (2 * HD) + j * HD, HD)
                            sp.dma_start(v_sb[j][:, 0:ST - 1, :], v_dram[bass.ds(b * S, (ST - 1) * P), cols].rearrange("(t p) d -> p t d", p=P)).then_inc(v_in[j], 16)
                            sp.dma_start(v_sb[j][0:SLAST, ST - 1, :], v_dram[bass.ds(b * S + (ST - 1) * P, SLAST), cols]).then_inc(v_in[j], 16)

        @block.gpsimd
        def _(pool):
            nc.gpsimd.memset(neg_mask[:, :, S:SPAD], FMAX).then_inc(pad_done, 1)
            for k in k_sb:
                nc.gpsimd.memset(k[:, S:SPAD].bitcast(F32), 0.0).then_inc(pad_done, 1)
            for lt in range(2):
                pool.sem_inc(mask_free[lt], 1)

            def negate(a, lt):
                pool.wait_ge(mask_in[lt], a * 16 + 16)
                nc.gpsimd.tensor_scalar(neg_mask[:, lt, 0:S], mask_raw[:, lt, :], -1.0, 0.0, ALU.mult, ALU.add).then_inc(mask_ready[lt], 4)
                pool.wait_ge(mask_ready[lt], a * 4 + 4)
                pool.sem_inc(mask_free[lt], 1)

            def spread(step):
                pool.wait_ge(recip_done, step + 1)
                pool.wait_ge(mix_done, step + 2)
                pool.sem_inc(recip_seen, 1)
                nc.gpsimd.tensor_copy(recip[:], recip_col[:].unsqueeze(2).to_broadcast([P, ROWS, HD])).then_inc(wide_done, 1)

            for lt in range(2):
                negate(0, lt)
            with pool.Fori(0, NLQ - 1) as a:
                for i in range(KVH - 1):
                    spread(a * KVH + i)
                for lt in range(2):
                    pool.wait_ge(min_done, a * (2 * KVH * ROWS) + (2 * KVH * ROWS - 2 * G * (1 - lt)))
                    negate(a + 1, lt)
                spread(a * KVH + (KVH - 1))
            for i in range(KVH):
                spread((NLQ - 1) * KVH + i)

        @block.tensor
        def _(pe):
            pe.sem_inc(qk_done, 2 * 2 * ROWS)
            pe.sem_inc(mix_done, 2)
            pe.wait_ge(pad_done, 3)

            def scores(p, r, j):
                n = p * (2 * RP) + 2 * r
                par, lt, h = r // ROWS % 2, r % ROWS // G, r % G
                if r % ROWS == 0 and j == 0:
                    pe.wait_ge(qk_in[par], p * 96 + (r // RP * 96 + 96))
                if not (isinstance(p, int) and p == 0 and r == 0):
                    pe.wait_ge(min_done, n + (j - 1))
                s0, s1, w = HALVES[j]
                for c, start in enumerate((s0, s1)):
                    last = nc.tensor.matmul(score[j][:, c, 0:w], q_sb[par][:, h, lt * P:(lt + 1) * P], k_sb[par][:, start:start + w], start=True, stop=True)
                last.then_inc(qk_done, 1)

            def turn(p, r, g, first):
                row = p * RP + r
                if g == 0:
                    pe.wait_ge(exp_done, row + 1)
                if g == 3 or not first:
                    sem_, n = ((copied_dve, row * 2), (copied_act, row * 2 - 1), (copied_act, row * 2), (copied_dve, row * 2 + 1))[g]
                    pe.wait_ge(sem_, n)
                bank = turned[g % 3]
                for k, st in enumerate(range(*GROUPS[g])):
                    w = min(P, S - st * P)
                    last = nc.tensor.transpose(bank[0:w, k, :], weights[r % 4][:, st * P:st * P + w], ident[:])
                last.then_inc(turn_done, 1)

            def mix(step, par, pair, first, sts):
                for st in sts:
                    if st == 0:
                        pe.wait_ge(v_in[par], pair * 32 + 32)
                        pe.wait_ge(copied_dve, step * (2 * ROWS) + 2 * ROWS)
                        pe.wait_ge(copied_act, step * (2 * ROWS) + 2 * ROWS)
                        if not first:
                            pe.wait_ge(norm_done, step)
                    w = min(P, S - st * P)
                    for h in range(G):
                        nc.tensor.matmul(mixed[h * HD:(h + 1) * HD, 0, :], v_sb[par][0:w, st, :], w_t[par][0:w, st, h, :], start=(st == 0), stop=(st == ST - 1))

            def spread(step):
                pe.wait_ge(wide_done, step + 1)
                for lt in range(LQ // P):
                    last = nc.tensor.transpose(mixed[:, 1, lt * P:(lt + 1) * P], recip[:, lt * G:(lt + 1) * G, :].rearrange("p h d -> p (h d)"), ident[:])
                last.then_inc(mix_done, 1)

            def pair(p, first=False, last=False):
                for r in range(RP):
                    for g in (0, 1):
                        turn(p, r, g, first and r == 0)
                    if not (last and r + AHEAD >= RP):
                        scores(p, r + AHEAD, 1)
                    for g in (2, 3):
                        turn(p, r, g, first and r == 0)
                    if not (last and r + AHEAD + 1 >= RP):
                        scores(p, r + AHEAD + 1, 0)
                    i, s = r // ROWS, r % ROWS
                    if s and not (first and i == 0):
                        step, par = p * 2 + (i - 1), 1 - i
                        pr = p if i else p - 1
                        mix(step, par, pr, first, range(2 * s - 2, min(2 * s, ST)))
                        if s == ROWS - 1:
                            spread(step)

            for r in range(AHEAD):
                for j in range(2):
                    scores(0, r, j)
            scores(0, AHEAD, 0)
            pair(0, first=True)
            with pe.Fori(1, PAIRS - 1) as p:
                pair(p)
            pair(PAIRS - 1, last=True)
            mix(NSTEP - 1, 1, PAIRS - 1, False, range(ST))
            spread(NSTEP - 1)

        @block.vector
        def _(dve):
            dve.wait_ge(pad_done, 3)

            def masked(p, r, j):
                n = p * (2 * RP) + 2 * r
                lt = r % ROWS // G
                if r % G == 0 and j == 0:
                    dve.wait_ge(mask_ready[lt], p + (r // RP + 1))
                if j == 0 and not (isinstance(p, int) and p == 0 and r < 4):
                    dve.wait_ge(turn_done, p * (4 * RP) + 4 * (r - 3))
                dve.wait_ge(qk_done, n + (j + 1 + 4 * ROWS))
                if j:
                    dve.wait_ge(min_done, n + 1)
                dve.sem_inc(half_seen, 1)
                s0, _, w = HALVES[j]
                nc.vector.tensor_tensor_reduce(
                    weights[r % 4][:, s0:s0 + 2 * w].rearrange("p (c s) -> p c s", c=2), score[j][:, :, 0:w],
                    neg_mask[:, lt, s0:s0 + 2 * w].rearrange("p (c s) -> p c s", c=2), 1.0,
                    row_min[:, r % 4, 0:1] if j else FMAX, ALU.add, ALU.min, row_min[:, r % 4, j:j + 1]).then_inc(min_done, 1)

            def copy_out(p, r, g):
                i = r // ROWS
                row = p * RP + r
                if r % ROWS == 0 and g == 0:
                    dve.wait_ge(mix_done, p * 2 + (i + 1))
                dve.wait_ge(turn_done, row * 4 + (g + 1))
                lt, h = r % ROWS // G, r % G
                a, b = GROUPS[g]
                w = P if b < ST else SLAST
                nc.vector.tensor_copy(w_t[i][0:w, a:b, h, lt * P:(lt + 1) * P], turned[g % 3][0:w, 0:b - a, :]).then_inc(copied_dve, 1)

            def reciprocals(step, par):
                dve.wait_ge(exp_done, step * ROWS + ROWS)
                if not (isinstance(step, int) and step == 0):
                    dve.wait_ge(wide_done, step)
                nc.vector.reciprocal(recip_col[:], denom[par][:]).then_inc(recip_done, 1)

            def normalise(step, par, pair):
                dve.wait_ge(recip_t_done, step + 1)
                dve.wait_ge(stored[par], pair * 16 + 32)
                nc.vector.tensor_tensor(attended[par][:], mixed[:, 0, :], recip_t[:], ALU.mult).then_inc(norm_done, 1)

            def pair(p, first=False, last=False):
                for r in range(RP):
                    i, s = r // ROWS, r % ROWS
                    ahead = not (last and r + AHEAD >= RP)
                    if ahead:
                        masked(p, r + AHEAD, 0)
                    copy_out(p, r, 0)
                    if ahead:
                        masked(p, r + AHEAD, 1)
                    copy_out(p, r, 3)
                    if s == 0 and not first:
                        normalise(p * 2 + (i - 2), i, p - 1)
                    if s == 1 and not (first and i == 0):
                        reciprocals(p * 2 + (i - 1), 1 - i)

            for r in range(AHEAD):
                for j in range(2):
                    masked(0, r, j)
            pair(0, first=True)
            with dve.Fori(1, PAIRS - 1) as p:
                pair(p)
            pair(PAIRS - 1, last=True)
            normalise(NSTEP - 2, 0, PAIRS - 1)
            reciprocals(NSTEP - 1, 1)
            normalise(NSTEP - 1, 1, PAIRS - 1)

        @block.scalar
        def _(act):
            for i in range(2):
                act.sem_inc(stored[i], 32)

            def exponents(p, r):
                i, s = r // ROWS % 2, r % ROWS
                if s == 0 and not (isinstance(p, int) and p == 0 and r < RP):
                    act.wait_ge(recip_done, p * 2 + (r // ROWS - 1))
                act.wait_ge(min_done, p * (2 * RP) + (2 * r + 2))
                row = weights[r % 4][:, 0:S]
                nc.scalar.activation(row, row, ACT.Exp, bias=row_min[:, r % 4, 1:2], scale=-1.0, accum_out=denom[i][:, s:s + 1]).then_inc(exp_done, 1)

            def copy_out(p, r, g):
                i = r // ROWS
                if r % ROWS == 0 and g == 1:
                    act.wait_ge(mix_done, p * 2 + (i + 1))
                act.wait_ge(turn_done, p * (4 * RP) + (4 * r + g + 1))
                lt, h = r % ROWS // G, r % G
                a, b = GROUPS[g]
                nc.scalar.copy(w_t[i][:, a:b, h, lt * P:(lt + 1) * P], turned[g % 3][:, 0:b - a, :]).then_inc(copied_act, 1)

            def copy_reciprocals(step):
                act.wait_ge(mix_done, step + 3)
                nc.scalar.copy(recip_t[:], mixed[:, 1, :]).then_inc(recip_t_done, 1)

            def store(step, par):
                act.wait_ge(norm_done, step + 1)
                act.dma_start(a_dram[bass.ds(step, 1)].rearrange("a p l -> (a p) l"), attended[par][:]).then_inc(stored[par], 16)

            def pair(p, first=False, last=False):
                for r in range(RP):
                    i, s = r // ROWS, r % ROWS
                    if not (last and r + 1 >= RP):
                        exponents(p, r + 1)
                    for g in (1, 2):
                        copy_out(p, r, g)
                    if s == 0 and not first:
                        copy_reciprocals(p * 2 + (i - 2))
                    if s == 3 and not first:
                        store(p * 2 + (i - 2), i)

            exponents(0, 0)
            pair(0, first=True)
            with act.Fori(1, PAIRS - 1) as p:
                pair(p)
            pair(PAIRS - 1, last=True)
            for i in range(2):
                copy_reciprocals(NSTEP - 2 + i)
                store(NSTEP - 2 + i, i)
            for i in range(2):
                act.wait_ge(stored[i], 32 + 16 * PAIRS)


def output(nc, x_flat, wo, bo, gamma, beta, a_dram, out_flat):
    NT = LQ // P
    with ExitStack() as held:
        def sb(name, shape, dt=F32):
            return held.enter_context(nc.sbuf_tensor(name, shape, dt))

        def sem(name):
            return held.enter_context(nc.semaphore(name))

        wo_raw = sb("wo_raw", [P, KVH, H])
        wo_hi, wo_lo = sb("wo_hi", [P, KVH, H], F32R), sb("wo_lo", [P, KVH, H], F32R)
        bo_row, gamma_row, beta_row = sb("bo_row", [P, H]), sb("gamma_row", [P, H]), sb("beta_row", [P, H])
        a_in = [sb(f"a_in{i}", [P, KVH, LQ]) for i in range(2)]
        a_hi = [sb(f"a_hi{i}", [P, KVH, LQ], F32R) for i in range(2)]
        a_lo = [sb(f"a_lo{i}", [P, KVH, LQ], F32R) for i in range(2)]
        resid = [sb(f"resid{i}", [P, H]) for i in range(NT)]
        total = [sb(f"total{i}", [P, H]) for i in range(NT)]
        stats = [sb(f"stats{i}", [P, 2, 6]) for i in range(NT)]
        moments = [sb(f"moments{i}", [P, 2]) for i in range(NT)]
        spread = [sb(f"spread{i}", [P, 2]) for i in range(NT)]
        eps = sb("eps", [P, 1])
        acc = [held.enter_context(nc.psum_tensor(f"acc{i}", [P, 2, 512], F32)) for i in range(NT)]

        w_in, rows_in = sem("wo_in"), sem("rows_const_in")
        w_hi_done, w_lo_done = sem("wo_hi_done"), sem("wo_lo_done")
        eps_done = sem("eps_done")
        a_landed = [sem(f"a_landed{i}") for i in range(2)]
        a_hi_done, a_lo_done = sem("a_hi_done"), sem("a_lo_done")
        x_landed = [sem(f"x_landed{i}") for i in range(NT)]
        resid_done = sem("resid_done")
        proj_done = sem("proj_done")
        total_done = sem("total_done")
        chain = sem("chain")
        stats_seen = sem("stats_seen")
        std_done = sem("std_done")
        recip_done = sem("std_recip_done")
        scaled = sem("scaled")
        final = sem("final")
        stored = sem("out_stored")
        free = [sem(f"total_free{i}") for i in range(NT)]

        block = held.enter_context(nc.Block())

        @block.sync
        def _(sp):
            sp.dma_start(wo_raw[:], wo.rearrange("(t p) n -> p t n", p=P)).then_inc(w_in, 16)
            for row, src in ((bo_row, bo), (gamma_row, gamma), (beta_row, beta)):
                sp.dma_start(row[:], src.partition_broadcast(P)).then_inc(rows_in, 16)
            with sp.Fori(0, NLQ // 2) as i:
                for j in range(2):
                    sp.wait_ge(a_lo_done, i * 2 + (j + 1))
                    sp.dma_start(a_in[j][:], a_dram[bass.ds(i * (2 * KVH) + j * KVH, KVH)].rearrange("k p l -> p k l")).then_inc(a_landed[j], 16)
                    for t in range(NT):
                        sp.wait_ge(total_done, i * (2 * NT) + (j * NT + t + 1))
                        sp.dma_start(resid[t][:], x_flat[bass.ds(i * (2 * LQ) + (j * LQ + t * P), P), :]).then_inc(x_landed[t], 16)

        @block.tensor
        def _(pe):
            pe.sem_inc(proj_done, 2 * NT)
            pe.wait_ge(w_lo_done, KVH)
            with pe.Fori(0, NLQ // 2) as i:
                for j in range(2):
                    pe.wait_ge(a_lo_done, i * 2 + (j + 3))
                    for t in range(NT):
                        pe.wait_ge(total_done, i * (2 * NT) + (j * NT + t + 1))
                        cols = slice(t * P, (t + 1) * P)
                        for n in range(2):
                            out_cols = slice(n * 512, (n + 1) * 512)
                            terms = [(a, w, k) for a, w in ((a_hi[j], wo_hi), (a_lo[j], wo_hi), (a_hi[j], wo_lo)) for k in range(KVH)]
                            for m, (a, w, k) in enumerate(terms):
                                last = nc.tensor.matmul(acc[t][:, n, :], a[:, k, cols], w[:, k, out_cols], start=(m == 0), stop=(m == len(terms) - 1))
                        last.then_inc(proj_done, 1)

        @block.scalar
        def _(act):
            act.wait_ge(w_in, 16)
            for k in range(KVH):
                nc.scalar.copy(wo_hi[:, k, :], wo_raw[:, k, :]).then_inc(w_hi_done, 1)
            act.wait_ge(eps_done, 1)
            def split_hi(pair, j):
                act.wait_ge(a_landed[j], pair * 16 + 16)
                act.wait_ge(proj_done, (pair * 2 + j) * NT + NT)
                nc.scalar.copy(a_hi[j][:], a_in[j][:]).then_inc(a_hi_done, 1)

            def deviations(pair, j):
                for t in range(NT):
                    act.wait_ge(chain, ((pair * 2 + j) * NT + (t + 1)) * 3)
                    nc.scalar.activation(spread[t][:, 0:1], moments[t][:, 1:2], ACT.Sqrt, bias=eps[:]).then_inc(std_done, 1)

            split_hi(0, 0)
            with act.Fori(0, NLQ // 2 - 1) as i:
                split_hi(i, 1)
                deviations(i, 0)
                split_hi(i + 1, 0)
                deviations(i, 1)
            split_hi(NLQ // 2 - 1, 1)
            deviations(NLQ // 2 - 1, 0)
            deviations(NLQ // 2 - 1, 1)

        @block.vector
        def _(dve):
            dve.sem_inc(a_lo_done, 2)
            dve.sem_inc(total_done, NT)
            for k in range(KVH):
                dve.wait_ge(w_hi_done, k + 1)
                nc.vector.tensor_tensor(wo_lo[:, k, :], wo_raw[:, k, :], wo_hi[:, k, :].bitcast(F32), ALU.subtract).then_inc(w_lo_done, 1)
            def split_lo(i, j):
                dve.wait_ge(a_hi_done, i * 2 + (j + 1))
                nc.vector.tensor_tensor(a_lo[j][:], a_in[j][:], a_hi[j][:].bitcast(F32), ALU.subtract).then_inc(a_lo_done, 1)

            def norm(i, j):
                for t in range(NT):
                    n = i * (2 * NT) + (j * NT + t)
                    dve.wait_ge(proj_done, n + (2 * NT + 1))
                    dve.wait_ge(resid_done, n + 1)
                    dve.wait_ge(free[t], i * 2 + (j + 1))
                    nc.vector.tensor_tensor(total[t][:].rearrange("p (c n) -> p c n", c=2), acc[t][:], resid[t][:].rearrange("p (c n) -> p c n", c=2), ALU.add).then_inc(total_done, 1)
                    dve.wait_ge(total_done, n + (NT + 1))
                    for c in range(2):
                        nc.vector.bn_stats(stats[t][:, c, :], total[t][:, c * 512:(c + 1) * 512]).then_inc(chain, 1)
                    dve.wait_ge(chain, n * 3 + 2)
                    dve.sem_inc(stats_seen, 1)
                    nc.vector.bn_aggr(moments[t][:], stats[t][:].rearrange("p c s -> p (c s)")).then_inc(chain, 1)
                    dve.wait_ge(std_done, n + 1)
                    nc.vector.reciprocal(spread[t][:, 1:2], spread[t][:, 0:1]).then_inc(recip_done, 1)
                    dve.wait_ge(recip_done, n + 1)
                    nc.vector.tensor_scalar(total[t][:], total[t][:], moments[t][:, 0:1], spread[t][:, 1:2], ALU.subtract, ALU.mult).then_inc(scaled, 1)
                    dve.wait_ge(scaled, n * 2 + 1)
                    nc.vector.tensor_tensor(total[t][:], total[t][:], gamma_row[:], ALU.mult).then_inc(scaled, 1)

            split_lo(0, 0)
            with dve.Fori(0, NLQ // 2 - 1) as i:
                split_lo(i, 1)
                norm(i, 0)
                split_lo(i + 1, 0)
                norm(i, 1)
            split_lo(NLQ // 2 - 1, 1)
            norm(NLQ // 2 - 1, 0)
            norm(NLQ // 2 - 1, 1)

        @block.gpsimd
        def _(pool):
            nc.gpsimd.memset(eps[:], EPS).then_inc(eps_done, 1)
            for t in range(NT):
                pool.sem_inc(free[t], 1)
            pool.wait_ge(rows_in, 48)

            def add_bias(i, j, t):
                pool.wait_ge(x_landed[t], i * 32 + (j * 16 + 16))
                nc.gpsimd.tensor_tensor(resid[t][:], resid[t][:], bo_row[:], ALU.add).then_inc(resid_done, 1)

            with pool.Fori(0, NLQ // 2) as i:
                for j in range(2):
                    for t in range(NT):
                        add_bias(i, j, t)
                    for t in range(NT):
                        n = i * (2 * NT) + (j * NT + t)
                        pool.wait_ge(scaled, n * 2 + 2)
                        nc.gpsimd.tensor_tensor(total[t][:], total[t][:], beta_row[:], ALU.add).then_inc(final, 1)
                        pool.wait_ge(final, n + 1)
                        pool.dma_start(out_flat[bass.ds(i * (2 * LQ) + (j * LQ + t * P), P), :], total[t][:]).then_inc(stored, 16)
                        pool.wait_ge(stored, n * 16 + 16)
                        pool.sem_inc(free[t], 1)


_INS = ["x", "ctx_2048", "mask_Bx1xSxS2_ff0"] + ["L0_xattn_" + n for n in ("Wq", "bq", "Wk", "bk", "Wv", "bv", "Wo", "bo", "gamma", "beta")]


def kernel(**inputs):
    import concourse.bacc as bacc
    from concourse.bass_utils import run_bass_kernel_spmd

    nc = bacc.Bacc("TRN2", target_bir_lowering=False, num_devices=1)
    arrays, args = {}, []
    for name in _INS:
        a = np.ascontiguousarray(inputs[name])
        arrays[f"in_{name}"] = a
        args.append(nc.dram_tensor(f"in_{name}", a.shape, mybir.dt.from_np(a.dtype), kind="ExternalInput").ap())
    out = nc.dram_tensor("out", (B, L, H), F32, kind="ExternalOutput").ap()
    xattn_program(nc, *args, out)
    r = run_bass_kernel_spmd(nc, [arrays], core_ids=[0])
    return r.results[0]["out"]
```

```python
from contextlib import ExitStack

import numpy as np

import concourse.bass as bass
from concourse import mybir

F32 = mybir.dt.float32
F32R = mybir.dt.float32r
ALU = mybir.AluOpType
ACT = mybir.ActivationFunctionType

P = 128
B, L, H = 4, 1024, 1024
S = 1601
NH, KVH, HD = 32, 8, 32
G = NH // KVH
KV = KVH * HD
KT = H // P
SCALE = float(HD) ** -0.5
EPS = 1e-6

XC = 512
NXC = B * L // XC
CC = 402
CSTART = (0, 400, 800, S - CC)
NCC = len(CSTART)
VSUB = (0, 128, 256, CC - P)
LQ = 512
NLQ = B * L // LQ
NSTEP = NLQ * KVH
ST = -(-S // P)
SLAST = S - (ST - 1) * P
STACK = 3 * HD
SHIFT = STACK + 3
OQ = 256
MT = B * L // P
FMAX = 3.0e38
FAR = 1.0e37


SPAD = 1604
HALVES = ((0, 400, 400), (800, 1202, 402))


def xattn_program(nc, x, ctx_kv, mask, wq, bq, wk, bk, wv, bv, wo, bo, gamma, beta, out):
    x_flat = x.rearrange("b l h -> (b l) h")
    ctx_flat = ctx_kv.rearrange("b s h -> (b s) h")
    mask_flat = mask.rearrange("b o l s -> (b o l) s")
    out_flat = out.rearrange("b l h -> (b l) h")

    q_dram = nc.dram_tensor("q_parts", [NLQ, KVH, 2, P, LQ], F32, kind="Internal").ap()
    k_dram = nc.dram_tensor("k_parts", [B, 2, KV, S], F32, kind="Internal").ap()
    v_dram = nc.dram_tensor("v_rows", [B * S, KV], F32, kind="Internal").ap()
    a_dram = nc.dram_tensor("weighted", [NSTEP, P, LQ], F32, kind="Internal").ap()
    d_dram = nc.dram_tensor("denominators", [NSTEP, G, LQ], F32, kind="Internal").ap()
    r_dram = nc.dram_tensor("reciprocals", [NSTEP, G, LQ], F32, kind="Internal").ap()

    with ExitStack() as whole:
        ident = whole.enter_context(nc.sbuf_tensor("ident", [P, P], F32))
        mask_sum = whole.enter_context(nc.sbuf_tensor("mask_sum", [P, MT], F32))
        project(nc, x_flat, ctx_flat, mask_flat, wq, bq, wk, bk, wv, bv, q_dram, k_dram, v_dram, ident, mask_sum)
        attend(nc, mask_flat, q_dram, k_dram, v_dram, a_dram, d_dram, ident, mask_sum)
        output(nc, x_flat, wo, bo, gamma, beta, a_dram, d_dram, r_dram, out_flat)


def project(nc, x_flat, ctx_flat, mask_flat, wq, bq, wk, bk, wv, bv, q_dram, k_dram, v_dram, ident, mask_sum):
    with ExitStack() as held:
        def sb(name, shape, dt=F32):
            return held.enter_context(nc.sbuf_tensor(name, shape, dt))

        def sem(name):
            return held.enter_context(nc.semaphore(name))

        wq_hi, wq_lo = sb("wq_hi", [P, KT, H], F32R), sb("wq_lo", [P, KT, H], F32R)
        wk_hi, wk_lo = sb("wk_hi", [P, KT, KV], F32R), sb("wk_lo", [P, KT, KV], F32R)
        wv_hi, wv_lo = sb("wv_hi", [P, KT, KV], F32R), sb("wv_lo", [P, KT, KV], F32R)
        bq_col, bk_col = sb("bq_col", [P, KT]), sb("bk_col", [P, KV // P])
        bq_scaled = sb("bq_scaled", [P, KT])
        bv_row = sb("bv_row", [P, KV])

        with ExitStack() as staging:
            w_raw = staging.enter_context(nc.sbuf_tensor("w_raw", [P, KT, H], F32))
            kv_raw = staging.enter_context(nc.sbuf_tensor("kv_raw", [P, 2, KT, KV], F32))
            wq_in, wk_in, wv_in, bias_in = (staging.enter_context(nc.semaphore(n)) for n in ("wq_in", "wk_in", "wv_in", "bias_in"))
            w_hi_done, w_lo_done = (staging.enter_context(nc.semaphore(n)) for n in ("w_hi_done", "w_lo_done"))
            ident_zero, ident_done = (staging.enter_context(nc.semaphore(n)) for n in ("ident_zero", "ident_done"))
            parts = (
                (wq_in, w_raw[:], wq_hi, wq_lo),
                (wk_in, kv_raw[:, 0], wk_hi, wk_lo),
                (wv_in, kv_raw[:, 1], wv_hi, wv_lo),
            )
            block = staging.enter_context(nc.Block())

            @block.sync
            def _(sp):
                sp.dma_start(w_raw[:], wq.rearrange("(t p) n -> p t n", p=P)).then_inc(wq_in, 16)
                sp.dma_start(kv_raw[:, 0], wk.rearrange("(t p) n -> p t n", p=P)).then_inc(wk_in, 16)
                sp.dma_start(kv_raw[:, 1], wv.rearrange("(t p) n -> p t n", p=P)).then_inc(wv_in, 16)
                with nc.allow_non_contiguous_dma(reason="biases by column"):
                    sp.dma_start(bq_col[:], bq.rearrange("(c p) -> p c", p=P)).then_inc(bias_in, 16)
                    sp.dma_start(bk_col[:], bk.rearrange("(c p) -> p c", p=P)).then_inc(bias_in, 16)
                sp.dma_start(bv_row[:], bv.partition_broadcast(P)).then_inc(bias_in, 16)

            @block.scalar
            def _(act):
                for raw_in, raw, hi, _ in parts:
                    act.wait_ge(raw_in, 16)
                    for t in range(KT):
                        nc.scalar.copy(hi[:, t, :], raw[:, t, :]).then_inc(w_hi_done, 1)

            @block.vector
            def _(dve):
                n = 0
                for _, raw, hi, lo in parts:
                    for t in range(KT):
                        n += 1
                        dve.wait_ge(w_hi_done, n)
                        nc.vector.tensor_tensor(lo[:, t, :], raw[:, t, :], hi[:, t, :].bitcast(F32), ALU.subtract).then_inc(w_lo_done, 1)
                dve.wait_ge(bias_in, 48)
                nc.vector.tensor_scalar(bq_scaled[:], bq_col[:], SCALE, None, ALU.mult).then_inc(w_lo_done, 1)
                dve.wait_ge(w_lo_done, 3 * KT + 1)

            @block.gpsimd
            def _(pool):
                nc.gpsimd.memset(ident[:], 0.0).then_inc(ident_zero, 1)
                pool.wait_ge(ident_zero, 1)
                nc.gpsimd.affine_select(out=ident[:], in_=ident[:], compare_op=ALU.not_equal, fill=1.0, base=0,
                                        pattern=[[-1, P]], channel_multiplier=1).then_inc(ident_done, 1)
                pool.wait_ge(ident_done, 1)

        MPC = MT // (B * NCC)
        rows = sb("rows", [P, XC // P, H])
        t_hi = [sb(f"t_hi{i}", [P, KT, XC], F32R) for i in range(2)]
        t_lo = [sb(f"t_lo{i}", [P, KT, XC], F32R) for i in range(2)]
        full = [sb(f"full{i}", [P, XC]) for i in range(2)]
        o_hi = [sb(f"o_hi{i}", [P, XC], F32R) for i in range(2)]
        o_lo = [sb(f"o_lo{i}", [P, XC], F32R) for i in range(2)]
        v_out = [sb(f"v_out{i}", [P, KV]) for i in range(2)]
        mask_tile = [sb(f"mask_tile{i}", [P, S]) for i in range(MPC)]
        turned = [held.enter_context(nc.psum_tensor(f"turned{i}", [P, XC], F32)) for i in range(2)]
        summed = [held.enter_context(nc.psum_tensor(f"summed{i}", [P, XC], F32)) for i in range(4)]

        rows_in = sem("rows_in")
        turn_done = sem("turn_done")
        hi_done = sem("hi_done")
        lo_done = sem("lo_done")
        sum_done = sem("sum_done")
        sum_read = sem("sum_read")
        part_hi = sem("part_hi")
        part_lo = sem("part_lo")
        part_stored = sem("part_stored")
        v_stored = sem("v_stored")
        mask_in = sem("mask_tile_in")
        mask_summed = sem("mask_summed")
        mask_seen = sem("mask_seen")
        part_free = [sem(f"part_free{i}") for i in range(2)]
        v_free = [sem(f"v_free{i}") for i in range(2)]

        XG, CG = KT, KV // P + len(VSUB)
        NX_SLICE, NX_SUM, NX_PART = NXC * KT, NXC * XG, NXC * XG // 2

        def slices(kind, c):
            return c * KT if kind == "x" else c * KT + NX_SLICE

        def sums(kind, c):
            return c * XG if kind == "x" else c * CG + NX_SUM

        def landed(kind, c):
            return c * 16 + 16 if kind == "x" else c * 32 + (16 * NXC + 32)

        def width(kind):
            return XC if kind == "x" else CC

        block = held.enter_context(nc.Block())

        @block.sync
        def _(sp):
            def load_x(c):
                sp.dma_start(rows[:], x_flat[bass.ds(c * XC, XC), :].rearrange("(t p) h -> p t h", p=P)).then_inc(rows_in, 16)

            load_x(0)
            with sp.Fori(1, NXC) as c:
                sp.wait_ge(turn_done, c * KT)
                load_x(c)
            with sp.Fori(0, B) as b:
                for n, start in enumerate(CSTART):
                    sp.wait_ge(turn_done, b * (NCC * KT) + (NX_SLICE + n * KT))
                    sp.dma_start(rows[:, 0:3, :], ctx_flat[bass.ds(b * S + start, 3 * P), :].rearrange("(t p) h -> p t h", p=P)).then_inc(rows_in, 16)
                    sp.dma_start(rows[0:CC - 3 * P, 3, :], ctx_flat[bass.ds(b * S + (start + 3 * P), CC - 3 * P), :]).then_inc(rows_in, 16)

        @block.tensor
        def _(pe):
            pe.sem_inc(sum_done, 2 * XG)

            def turn(kind, c):
                n0 = slices(kind, c)
                pe.wait_ge(rows_in, landed(kind, c))
                for t in range(KT):
                    pe.wait_ge(lo_done, n0 + (t + 1))
                    for at in range(0, width(kind), P):
                        w = min(P, width(kind) - at)
                        last = nc.tensor.transpose(turned[t % 2][:, at:at + w], rows[0:w, at // P, t * P:(t + 1) * P], ident[0:w, 0:w])
                    last.then_inc(turn_done, 1)

            def three(acc, pairs):
                n = 0
                for lhs, rhs in pairs:
                    last = nc.tensor.matmul(acc, lhs, rhs, start=(n == 0), stop=(n == len(pairs) - 1))
                    n += 1
                last.then_inc(sum_done, 1)

            def multiply(kind, c, par):
                n0, g = sums(kind, c), 0
                off = 0 if kind == "x" else par * CG
                pe.wait_ge(lo_done, slices(kind, c) + (KT + 2))
                hi, lo = t_hi[par], t_lo[par]
                w_hi, w_lo, tiles = (wq_hi, wq_lo, KT) if kind == "x" else (wk_hi, wk_lo, KV // P)
                for ct in range(tiles):
                    pe.wait_ge(sum_read, n0 + (g + 1))
                    cols = slice(ct * P, (ct + 1) * P)
                    three(summed[(off + g) % 4][:, 0:width(kind)],
                          [(w[:, t, cols], m[:, t, 0:width(kind)]) for w, m in ((w_hi, hi), (w_hi, lo), (w_lo, hi)) for t in range(KT)])
                    g += 1
                if kind == "ctx":
                    for v0 in VSUB:
                        pe.wait_ge(sum_read, n0 + (g + 1))
                        three(summed[(off + g) % 4][:, 0:KV],
                              [(m[:, t, v0:v0 + P], w[:, t, :]) for m, w in ((hi, wv_hi), (lo, wv_hi), (hi, wv_lo)) for t in range(KT)])
                        g += 1

            turn("x", 0)
            with pe.Fori(0, NXC // 2 - 1) as i:
                for par in range(2):
                    turn("x", i * 2 + (par + 1))
                    multiply("x", i * 2 + par, par)
            turn("x", NXC - 1)
            multiply("x", NXC - 2, 0)
            turn("ctx", 0)
            multiply("x", NXC - 1, 1)
            with pe.Fori(0, B * NCC // 2 - 1) as i:
                for par in range(2):
                    turn("ctx", i * 2 + (par + 1))
                    multiply("ctx", i * 2 + par, par)
            turn("ctx", B * NCC - 1)
            multiply("ctx", B * NCC - 2, 0)
            multiply("ctx", B * NCC - 1, 1)

        @block.scalar
        def _(act):
            def split_hi(kind, c, par):
                n0 = slices(kind, c)
                before = c * XG + XG if kind == "x" else (c + 9) * XG if isinstance(c, int) and c < 2 else c * CG + (NX_SUM + 2 * XG - CG)
                act.wait_ge(sum_done, before)
                for t in range(KT):
                    act.wait_ge(turn_done, n0 + (t + 1))
                    nc.scalar.copy(t_hi[par][:, t, 0:width(kind)], turned[t % 2][:, 0:width(kind)]).then_inc(hi_done, 1)

            def parts_hi(kind, c, par):
                n0 = sums(kind, c) + 2 * XG
                off = 0 if kind == "x" else par * CG
                if kind == "ctx":
                    if not (isinstance(c, int) and c == 0):
                        act.wait_ge(mask_summed, c * MPC)
                    for j in range(MPC):
                        act.dma_start(mask_tile[j][:], mask_flat[bass.ds(c * (MPC * P) + j * P, P), :]).then_inc(mask_in, 16)
                for g in range(KT if kind == "x" else KV // P):
                    act.wait_ge(sum_done, n0 + (g + 1))
                    seq = c * (XG // 2) + g // 2 if kind == "x" else c + NX_PART
                    act.wait_ge(part_free[g % 2], seq + 1)
                    acc = summed[(off + g) % 4][:, 0:width(kind)]
                    if kind == "x":
                        ins = nc.scalar.activation(o_hi[g % 2][:, 0:XC], acc, ACT.Identity, bias=bq_scaled[:, g:g + 1], scale=SCALE)
                    else:
                        ins = nc.scalar.activation(o_hi[g % 2][:, 0:CC], acc, ACT.Identity, bias=bk_col[:, g:g + 1])
                    ins.then_inc(part_hi, 1)

            split_hi("x", 0, 0)
            with act.Fori(0, NXC // 2 - 1) as i:
                for par in range(2):
                    split_hi("x", i * 2 + (par + 1), 1 - par)
                    parts_hi("x", i * 2 + par, par)
            split_hi("x", NXC - 1, 1)
            parts_hi("x", NXC - 2, 0)
            split_hi("ctx", 0, 0)
            parts_hi("x", NXC - 1, 1)
            split_hi("ctx", 1, 1)
            parts_hi("ctx", 0, 0)
            with act.Fori(0, B * NCC // 2 - 1) as i:
                split_hi("ctx", i * 2 + 2, 0)
                parts_hi("ctx", i * 2 + 1, 1)
                split_hi("ctx", i * 2 + 3, 1)
                parts_hi("ctx", i * 2 + 2, 0)
            parts_hi("ctx", B * NCC - 1, 1)

        @block.vector
        def _(dve):
            dve.sem_inc(lo_done, 2)
            dve.sem_inc(sum_read, 4)

            def split_lo(kind, c, par):
                n0 = slices(kind, c)
                for t in range(KT):
                    dve.wait_ge(hi_done, n0 + (t + 1))
                    w = width(kind)
                    nc.vector.tensor_tensor(t_lo[par][:, t, 0:w], turned[t % 2][:, 0:w], t_hi[par][:, t, 0:w].bitcast(F32), ALU.subtract).then_inc(lo_done, 1)

            def parts_lo(kind, c, par):
                n0 = sums(kind, c)
                p0 = c * XG if kind == "x" else c * (KV // P) + NXC * XG
                off = 0 if kind == "x" else par * CG
                w, tiles = (XC, KT) if kind == "x" else (CC, KV // P)
                for g in range(tiles):
                    dve.wait_ge(part_hi, p0 + (g + 1))
                    acc = summed[(off + g) % 4][:, 0:w]
                    if kind == "x":
                        ins = nc.vector.tensor_scalar(full[g % 2][:, 0:w], acc, SCALE, bq_scaled[:, g:g + 1], ALU.mult, ALU.add)
                    else:
                        ins = nc.vector.tensor_scalar(full[g % 2][:, 0:w], acc, bk_col[:, g:g + 1], None, ALU.add)
                    ins.then_inc(sum_read, 1)
                    dve.wait_ge(sum_read, n0 + (g + 5))
                    nc.vector.tensor_tensor(o_lo[g % 2][:, 0:w], full[g % 2][:, 0:w], o_hi[g % 2][:, 0:w].bitcast(F32), ALU.subtract).then_inc(part_lo, 1)
                if kind == "ctx":
                    for j in range(len(VSUB)):
                        g = tiles + j
                        dve.wait_ge(sum_done, n0 + (g + 1 + 2 * XG))
                        dve.wait_ge(v_free[j % 2], c * 2 + (j // 2 + 1))
                        nc.vector.tensor_tensor(v_out[j % 2][:], summed[(off + g) % 4][:, 0:KV], bv_row[:], ALU.add).then_inc(sum_read, 1)
                    dve.wait_ge(mask_in, c * (16 * MPC) + 16 * MPC)
                    dve.sem_inc(mask_seen, MPC)
                    for j in range(MPC):
                        nc.vector.tensor_reduce(mask_sum[:, bass.ds(c * MPC + j, 1)], mask_tile[j][:], mybir.AxisListType.X, ALU.add, apply_absolute_value=True).then_inc(mask_summed, 1)

            split_lo("x", 0, 0)
            with dve.Fori(0, NXC // 2 - 1) as i:
                for par in range(2):
                    split_lo("x", i * 2 + (par + 1), 1 - par)
                    parts_lo("x", i * 2 + par, par)
            split_lo("x", NXC - 1, 1)
            parts_lo("x", NXC - 2, 0)
            split_lo("ctx", 0, 0)
            parts_lo("x", NXC - 1, 1)
            with dve.Fori(0, B * NCC // 2 - 1) as i:
                for par in range(2):
                    split_lo("ctx", i * 2 + (par + 1), 1 - par)
                    parts_lo("ctx", i * 2 + par, par)
            split_lo("ctx", B * NCC - 1, 1)
            parts_lo("ctx", B * NCC - 2, 0)
            parts_lo("ctx", B * NCC - 1, 1)
            dve.wait_ge(mask_summed, MT)

        @block.gpsimd
        def _(pool):
            for i in range(2):
                pool.sem_inc(part_free[i], 1)
                pool.sem_inc(v_free[i], 1)
            with pool.Fori(0, NXC) as c:
                for g in range(KT):
                    pool.wait_ge(part_lo, c * XG + (g + 1))
                    for n, part in enumerate((o_hi, o_lo)):
                        dst = q_dram[bass.ds(c, 1), g, n].rearrange("a p l -> (a p) l")
                        pool.dma_start(dst, part[g % 2][:].bitcast(F32)).then_inc(part_stored, 16)
                    pool.wait_ge(part_stored, c * (32 * XG) + 32 * (g + 1))
                    pool.sem_inc(part_free[g % 2], 1)
            with pool.Fori(0, B) as b:
                for n, start in enumerate(CSTART):
                    for g in range(KV // P):
                        seq = NXC * XG + n * (KV // P) + g + 1
                        pool.wait_ge(part_lo, b * (NCC * KV // P) + seq)
                        for m, part in enumerate((o_hi, o_lo)):
                            dst = k_dram[bass.ds(b, 1), m, g * P:(g + 1) * P, start:start + CC].rearrange("b p s -> (b p) s")
                            pool.dma_start(dst, part[g % 2][:, 0:CC].bitcast(F32)).then_inc(part_stored, 16)
                        pool.wait_ge(part_stored, b * (32 * NCC * KV // P) + 32 * seq)
                        pool.sem_inc(part_free[g % 2], 1)
                    for j, v0 in enumerate(VSUB):
                        pool.wait_ge(sum_read, b * (NCC * CG) + (NX_SUM + n * CG + KV // P + j + 1 + 4))
                        pool.dma_start(v_dram[bass.ds(b * S + (start + v0), P), :], v_out[j % 2][:]).then_inc(v_stored, 16)
                        pool.wait_ge(v_stored, b * (16 * NCC * len(VSUB)) + 16 * (n * len(VSUB) + j + 1))
                        pool.sem_inc(v_free[j % 2], 1)


def attend(nc, mask_flat, q_dram, k_dram, v_dram, a_dram, d_dram, ident, mask_sum):
    QUAD = 4
    NQUAD = NSTEP // QUAD
    NROW = G * LQ // P
    LEAD = 5
    PACE = [(1, 0, 1, int(st in (3, 5, 6, 8, 9, 10))) for st in range(ST)]
    LAG = 2
    POOL = (0, 1, 3, 4, 6, 7, 9, 10)
    REST = tuple(st for st in range(ST) if st not in POOL)
    RINGS = (4, 2)
    SUMS_AT = 2
    MIXED_AT, DENOM_AT = 2, 3
    TURN_AT = 10
    NPOOL = len(POOL) - 1
    QB = 4
    NLT = LQ // P
    NB = L // LQ

    def ring(st):
        return (POOL, RINGS[0], 0) if st in POOL else (REST, RINGS[1], RINGS[0])

    def buffer(s, st):
        tiles, size, first = ring(st)
        return first + (s * len(tiles) + tiles.index(st)) % size

    def tile_before(s, st):
        tiles, size, _ = ring(st)
        n = s * len(tiles) + tiles.index(st) - size
        return n // len(tiles), tiles[n % len(tiles)]

    with ExitStack() as held:
        def sb(name, shape, dt=F32):
            return held.enter_context(nc.sbuf_tensor(name, shape, dt))

        def sem(name):
            return held.enter_context(nc.semaphore(name))

        q_sb = [sb(f"q_sb{i}", [SHIFT, G, LQ], F32R) for i in range(QB)]
        k_sb = [sb(f"k_sb{i}", [SHIFT, SPAD], F32R) for i in range(QB)]
        v_sb = [sb(f"v_sb{i}", [P, ST, HD]) for i in range(QB)]
        mask_max = sb("mask_max", [P, NLT, SPAD])
        mask_exp = sb("mask_exp", [P, NLT, S])
        masked_row = [sb(f"masked_row{i}", [P, 2 * HALVES[i][2]]) for i in range(2)]
        half_max = sb("half_max", [P, 2])
        row_max = [sb(f"row_max{i}", [P, G, NLT]) for i in range(2)]
        rest = sb("rest", [P, NROW])
        parts = sb("parts", [P, 3, NROW], F32R)
        parts_t = sb("parts_t", [3 * NROW, P], F32R)
        weights = [sb(f"weights{i}", [P, G, LQ]) for i in range(sum(RINGS))]
        sum_pool = [sb(f"sum_pool{i}", [P, G, LQ]) for i in range(2)]
        ones = sb("ones", [P, HD])
        mixed_sb = [sb(f"mixed_sb{i}", [P, LQ]) for i in range(2)]
        denom_sb = [sb(f"denom_sb{i}", [P, LQ]) for i in range(2)]
        count = sb("count", [P, 1])
        flag = sb("flag", [1, 1], mybir.dt.int32)
        score = [held.enter_context(nc.psum_tensor(f"score{i}", [P, 2, 512], F32)) for i in range(2)]
        logit = [held.enter_context(nc.psum_tensor(f"logit{i}", [P, LQ], F32)) for i in range(2)]
        mixed = held.enter_context(nc.psum_tensor("mixed", [P, LQ], F32))
        denom = held.enter_context(nc.psum_tensor("denom", [P, LQ], F32))

        const_done = sem("const_done")
        count_done = sem("count_done")
        total_done = sem("count_total")
        flag_done = sem("flag_done")
        mask_in = [sem(f"mask_in{i}") for i in range(NLT)]
        mask_ready = [sem(f"mask_ready{i}") for i in range(NLT)]
        mask_exp_in = sem("mask_exp_in")
        mask_exp_seen = sem("mask_exp_seen")
        mask_exp_ready = sem("mask_exp_ready")
        qk_in = [sem(f"qk_in{i}") for i in range(QB)]
        v_in = [sem(f"v_in{i}") for i in range(QB)]
        score_done = sem("score_done")
        half_seen = sem("half_seen")
        max_done = sem("max_done")
        rest_done = sem("rest_done")
        parts_seen = sem("parts_seen")
        turn_done = sem("turn_done2")
        turn_copied = sem("turn_copied")
        shift_in = [sem(f"shift_in{i}") for i in range(QB)]
        logit_done = sem("logit_done")
        exp_done = sem("exp_done")
        pool_added = sem("pool_added")
        mix_done = sem("mix_done")
        mixed_copied = sem("mixed_copied")
        denom_done = sem("denom_done")
        denom_copied = sem("denom_copied")
        sync_seen = sem("sync_seen")
        mixed_stored = [sem(f"mixed_stored{i}") for i in range(2)]
        denom_stored = [sem(f"denom_stored{i}") for i in range(2)]

        LOGITS0, MIX0, MAX0 = QB * ST * G, QB * ST, 2 * NROW

        block = held.enter_context(nc.Block())

        @block.sync
        def _(sp):
            sp.wait_ge(flag_done, 1)
            any_mask = sp.value_load(flag[0:1, 0:1], min_val=0, max_val=1)

            def load_step(b, lq, n):
                a, j = b * NB + lq, n % QB
                step = a * KVH + n
                sp.wait_ge(logit_done, step * (ST * G) + ST * G)
                sp.sem_inc(sync_seen, 1)
                for r, part in enumerate((0, 1, 0)):
                    src = q_dram[bass.ds(a, 1), n, part].rearrange("a (h d) l -> (a d) h l", d=HD)
                    sp.dma_start(q_sb[j][r * HD:(r + 1) * HD].bitcast(F32), src).then_inc(qk_in[j], 16)
                for r, part in enumerate((0, 0, 1)):
                    src = k_dram[bass.ds(b, 1), part, n * HD:(n + 1) * HD, :].rearrange("b d s -> (b d) s")
                    sp.dma_start(k_sb[j][r * HD:(r + 1) * HD, 0:S].bitcast(F32), src).then_inc(qk_in[j], 16)
                sp.wait_ge(mix_done, step * ST + ST)
                sp.sem_inc(sync_seen, 1)
                cols = slice(n * HD, (n + 1) * HD)
                sp.dma_start(v_sb[j][:, 0:ST - 1, :], v_dram[bass.ds(b * S, (ST - 1) * P), cols].rearrange("(t p) d -> p t d", p=P)).then_inc(v_in[j], 16)
                sp.dma_start(v_sb[j][0:SLAST, ST - 1, :], v_dram[bass.ds(b * S + (ST - 1) * P, SLAST), cols]).then_inc(v_in[j], 16)

            def load_mask(a, lt):
                sp.wait_ge(max_done, a * (2 * NROW * KVH) + 2 * G * (lt + 1))
                sp.sem_inc(sync_seen, 1)
                sp.dma_start(mask_max[:, lt, 0:S], mask_flat[bass.ds(a * LQ + lt * P, P), :]).then_inc(mask_in[lt], 16)

            def mask_landed(a, lt):
                sp.wait_ge(mask_in[lt], a * 16 + 16)
                sp.sem_inc(mask_ready[lt], KVH // QUAD)

            def load_mask_exp(a):
                with sp.If(any_mask > 0):
                    sp.wait_ge(logit_done, a * (KVH * ST * G) + LOGITS0)
                    sp.sem_inc(sync_seen, 1)
                    for lt in range(NLT):
                        sp.dma_start(mask_exp[:, lt, :], mask_flat[bass.ds(a * LQ + lt * P, P), :]).then_inc(mask_exp_in, 16)

            def shift(step, j):
                sp.wait_ge(turn_copied, step + 1)
                sp.sem_inc(sync_seen, 1)
                for r in range(3):
                    sp.dma_start(q_sb[j][STACK + r:STACK + r + 1].bitcast(F32).rearrange("a h (t l) -> a (h t) l", l=P),
                                 parts_t[r * NROW:(r + 1) * NROW, :].bitcast(F32)).then_inc(shift_in[j], 16)

            def store(step, par):
                sp.wait_ge(mixed_copied, step + 1)
                sp.sem_inc(sync_seen, 1)
                sp.dma_start(a_dram[bass.ds(step, 1)].rearrange("a p l -> (a p) l"), mixed_sb[par][:]).then_inc(mixed_stored[par], 16)
                sp.wait_ge(denom_copied, step + 1)
                sp.sem_inc(sync_seen, 1)
                sp.dma_start(d_dram[bass.ds(step, 1)].rearrange("a h l -> (a h) l"), denom_sb[par][0:P:HD, :]).then_inc(denom_stored[par], 16)

            def batch(b, first=False, last=False):
                for lq in range(NB):
                    for n in range(KVH):
                        a = b * NB + lq
                        step = a * KVH + n
                        if n == 0:
                            load_mask_exp(a)
                        ahead = lq * KVH + n + 3
                        if ahead < NB * KVH:
                            load_step(b, ahead // KVH, ahead % KVH)
                        elif not last:
                            load_step(b + 1, 0, ahead % KVH)
                        if not (first and lq == 0 and n == 0):
                            store(step - 1, (n - 1) % 2)
                        final = last and lq == NB - 1
                        if n == KVH - 2 and not final:
                            for lt in range(NLT - 1):
                                load_mask(a + 1, lt)
                            for lt in range(2):
                                mask_landed(a + 1, lt)
                            load_mask(a + 1, NLT - 1)
                        if not (final and n == KVH - 1):
                            shift(step + 1, (n + 1) % QB)
                        if n == KVH - 2 and not final:
                            for lt in range(2, NLT):
                                mask_landed(a + 1, lt)

            load_step(0, 0, 0)
            for lt in range(NLT):
                load_mask(0, lt)
            load_step(0, 0, 1)
            for lt in range(NLT):
                mask_landed(0, lt)
            load_step(0, 0, 2)
            shift(0, 0)
            batch(0, first=True)
            with sp.Fori(1, B - 1) as b:
                batch(b)
            batch(B - 1, last=True)
            store(NSTEP - 1, 1)
            for i in range(2):
                sp.wait_ge(mixed_stored[i], 16 + 16 * (NSTEP // 2))
                sp.wait_ge(denom_stored[i], 16 + 16 * (NSTEP // 2))

        @block.gpsimd
        def _(pool):
            nc.gpsimd.memset(mask_max[:, :, S:SPAD], -FMAX).then_inc(const_done, 1)
            pool.wait_ge(const_done, 1)
            nc.gpsimd.memset(ones[:], 1.0).then_inc(const_done, 1)
            for i, k in enumerate(k_sb):
                pool.wait_ge(const_done, 2 + 2 * i)
                nc.gpsimd.memset(k[0:STACK, S:SPAD].bitcast(F32), 0.0).then_inc(const_done, 1)
                pool.wait_ge(const_done, 3 + 2 * i)
                nc.gpsimd.memset(k[STACK:SHIFT, :].bitcast(F32), 1.0).then_inc(const_done, 1)

            def add(quad, s, n):
                step, st = quad * QUAD + s, POOL[n + 1]
                pool.wait_ge(exp_done, quad * (QUAD * ST * G) + (s * ST + st + 1) * G)
                if n == 0:
                    pool.wait_ge(denom_done, step + 1)
                    first = weights[buffer(s, POOL[0])]
                else:
                    pool.wait_ge(pool_added, step * NPOOL + n)
                    first = sum_pool[s % 2]
                nc.gpsimd.tensor_tensor(sum_pool[s % 2][:], first[:], weights[buffer(s, st)][:], ALU.add).then_inc(pool_added, 1)

            pool.wait_ge(flag_done, 1)
            any_mask = pool.value_load(flag[0:1, 0:1], min_val=0, max_val=1)
            with pool.Fori(0, NLQ) as a:
                with pool.If(any_mask > 0):
                    pool.wait_ge(mask_exp_in, a * (16 * NLT) + 16 * NLT)
                    pool.sem_inc(mask_exp_seen, 1)
                    nc.gpsimd.tensor_scalar(mask_exp[:], mask_exp[:], -FAR, None, ALU.max).then_inc(mask_exp_ready, KVH // QUAD)
                for q in range(KVH // QUAD):
                    for s in range(QUAD):
                        for n in range(NPOOL):
                            add(a * (KVH // QUAD) + q, s, n)

        @block.tensor
        def _(pe):
            pe.sem_inc(logit_done, LOGITS0)
            pe.sem_inc(mix_done, MIX0)
            pe.sem_inc(denom_done, 2)
            pe.wait_ge(const_done, 2 + 2 * QB)
            pe.wait_ge(count_done, 1)
            nc.tensor.matmul(denom[0:1, 0:1], count[:], ones[:, 0:1], start=True, stop=True).then_inc(total_done, 1)

            def scores(quad, m, j):
                buf, k = m // NROW % QB, m % NROW
                lt, h = k // G, k % G
                if k == 0 and j == 0:
                    pe.wait_ge(qk_in[buf], quad * 96 + 96 * (m // (NROW * QUAD) + 1))
                if not (isinstance(quad, int) and quad * QUAD * NROW + m == 0):
                    pe.wait_ge(max_done, quad * (2 * QUAD * NROW) + (2 * m + j - 1 + MAX0))
                s0, s1, w = HALVES[j]
                for c, start in enumerate((s0, s1)):
                    last = nc.tensor.matmul(score[j][:, c, 0:w], q_sb[buf][0:STACK, h, lt * P:(lt + 1) * P], k_sb[buf][0:STACK, start:start + w], start=True, stop=True)
                last.then_inc(score_done, 1)

            def turn(quad, s):
                step = quad * QUAD + s
                pe.wait_ge(rest_done, step * 4 + 4)
                if not (isinstance(step, int) and step == 0):
                    pe.wait_ge(exp_done, quad * (QUAD * ST * G) + ((s - 1) * ST + TURN_AT + 1) * G)
                pe.sem_inc(parts_seen, 1)
                nc.tensor.transpose(logit[0][0:3 * NROW, 0:P], parts[:].bitcast(F32).rearrange("p a r -> p (a r)"), ident[:]).then_inc(turn_done, 1)

            def logits(quad, s, st, h, masked):
                n = (s * ST + st) * G + h
                if st == 0 and h == 0:
                    pe.wait_ge(shift_in[s], quad * 48 + 48)
                    if masked:
                        pe.wait_ge(mask_exp_ready, quad + 1)
                if not (isinstance(quad, int) and quad == 0 and n < 2):
                    pe.wait_ge(exp_done, quad * (QUAD * ST * G) + (n - 1))
                if st == TURN_AT + 1 and h == 0:
                    step = quad * QUAD + s
                    pe.wait_ge(turn_copied, NSTEP if isinstance(step, int) and step == NSTEP - 1 else step + 2)
                w = min(P, S - st * P)
                keys = slice(st * P, st * P + w)
                bank = logit[h % 2]
                if masked:
                    for lt in range(NLT):
                        nc.tensor.matmul(bank[0:w, lt * P:(lt + 1) * P], mask_exp[:, lt, keys], ident[:], start=(lt == 0), stop=False, skip_group_check=True)
                nc.tensor.matmul(bank[0:w, :], k_sb[s][:, keys], q_sb[s][:, h, :], start=not masked, stop=True, skip_group_check=masked).then_inc(logit_done, 1)

            def sum_heads(out, lhs, rhs, w, start, stop):
                for h in range(G):
                    last = nc.tensor.matmul(out[h * HD:(h + 1) * HD, :], lhs, rhs[0:w, h, :], start=start, stop=stop)
                return last

            def mix(quad, tile):
                s, st = tile // ST % QUAD, tile % ST
                if st == 0:
                    pe.wait_ge(v_in[s], quad * 32 + 32)
                    if not (isinstance(quad, int) and quad * QUAD + s == 0):
                        pe.wait_ge(mixed_copied, quad * QUAD + s)
                pe.wait_ge(exp_done, quad * (QUAD * ST * G) + (tile + 1) * G)
                w = min(P, S - st * P)
                last = sum_heads(mixed, v_sb[s][0:w, st, :], weights[buffer(s, st)], w, st == 0, st == ST - 1)
                if st not in REST:
                    last.then_inc(mix_done, 1)

            def total(quad, tile):
                s, st = tile // ST % QUAD, tile % ST
                if st == REST[0] and not (isinstance(quad, int) and quad * QUAD + s == 0):
                    pe.wait_ge(denom_copied, quad * QUAD + s)
                w = min(P, S - st * P)
                sum_heads(denom, ones[0:w, :], weights[buffer(s, st)], w, st == REST[0], False).then_inc(mix_done, 1)

            def denominators(step, par):
                pe.wait_ge(pool_added, step * NPOOL + NPOOL)
                sum_heads(denom, ones[:], sum_pool[par], P, False, True).then_inc(denom_done, 1)

            def quad_steps(quad, masked, first=False, last=False):
                for s in range(QUAD):
                    k = 0
                    for st in range(ST):
                        tile = s * ST + st
                        for h in range(G):
                            logits(quad, s, st, h, masked)
                            if h == 1:
                                if st == SUMS_AT and not (first and s == 0):
                                    denominators(quad * QUAD + (s - 1), (s - 1) % 2)
                                if not (first and tile < LAG):
                                    mix(quad, tile - LAG)
                            if h == G - 1:
                                if (tile - LAG) % ST in REST and not (first and tile < LAG):
                                    total(quad, tile - LAG)
                                if st == TURN_AT and not (last and s == QUAD - 1):
                                    turn(quad, s + 1)
                            for _ in range(PACE[st][h]):
                                m = NROW * (s + 1) + LEAD + k // 2
                                if not (last and m >= QUAD * NROW):
                                    scores(quad, m, k % 2)
                                k += 1

            def steps(masked):
                for m in range(NROW + LEAD):
                    for j in range(2):
                        scores(0, m, j)
                    if m == NROW + 1:
                        turn(0, 0)
                quad_steps(0, masked, first=True)
                with pe.Fori(1, NQUAD - 1) as quad:
                    quad_steps(quad, masked)
                quad_steps(NQUAD - 1, masked, last=True)
                for tile in range(QUAD * ST - LAG, QUAD * ST):
                    mix(NQUAD - 1, tile)
                    total(NQUAD - 1, tile)
                denominators(NSTEP - 1, 1)

            pe.wait_ge(flag_done, 1)
            any_mask = pe.value_load(flag[0:1, 0:1], min_val=0, max_val=1)
            with pe.If(any_mask > 0):
                steps(True)
            with pe.Else():
                steps(False)

        @block.vector
        def _(dve):
            dve.sem_inc(max_done, MAX0)
            nc.vector.tensor_reduce(count[:], mask_sum[:], mybir.AxisListType.X, ALU.add).then_inc(count_done, 1)
            dve.wait_ge(total_done, 1)
            nc.vector.tensor_scalar(flag[:], denom[0:1, 0:1], 0.0, None, ALU.not_equal).then_inc(flag_done, 1)
            dve.wait_ge(const_done, 2 + 2 * QB)

            def maxima(quad, m, j):
                k = m % NROW
                lt, h = k // G, k % G
                n = quad * (2 * QUAD * NROW) + 2 * m
                if h == 0 and j == 0:
                    dve.wait_ge(mask_ready[lt], quad + (m // (QUAD * NROW) + 1))
                dve.wait_ge(score_done, n + (j + 1))
                if j:
                    dve.wait_ge(max_done, n + (1 + MAX0))
                dve.sem_inc(half_seen, 1)
                s0, _, w = HALVES[j]
                half, whole = half_max[:, m % 2:m % 2 + 1], row_max[m // NROW % 2][:, h, lt:lt + 1]
                nc.vector.tensor_tensor_reduce(
                    masked_row[j][:].rearrange("p (c s) -> p c s", c=2), score[j][:, :, 0:w],
                    mask_max[:, lt, s0:s0 + 2 * w].rearrange("p (c s) -> p c s", c=2), 1.0,
                    half if j else -FMAX, ALU.add, ALU.max, whole if j else half).then_inc(max_done, 1)

            def split(step, par):
                top = row_max[par][:].rearrange("p h t -> p (h t)")
                dve.wait_ge(max_done, step * (2 * NROW) + (2 * NROW + MAX0))
                if not (isinstance(step, int) and step == 0):
                    dve.wait_ge(turn_done, step)
                nc.vector.tensor_scalar(parts[:, 0, :], top, -1.0, None, ALU.mult).then_inc(rest_done, 1)
                dve.wait_ge(rest_done, step * 4 + 1)
                nc.vector.scalar_tensor_tensor(out=rest[:], in0=top, scalar=-1.0, in1=parts[:, 0, :].bitcast(F32), op0=ALU.mult, op1=ALU.subtract).then_inc(rest_done, 1)
                dve.wait_ge(rest_done, step * 4 + 2)
                nc.vector.tensor_scalar(parts[:, 1, :], rest[:], 1.0, None, ALU.mult).then_inc(rest_done, 1)
                dve.wait_ge(rest_done, step * 4 + 3)
                nc.vector.tensor_tensor(parts[:, 2, :], rest[:], parts[:, 1, :].bitcast(F32), ALU.subtract).then_inc(rest_done, 1)

            def quad_steps(quad, first=False, last=False):
                for s in range(QUAD):
                    for k in range(2 * NROW):
                        m = NROW * (s + 1) + LEAD + k // 2
                        if not (last and m >= QUAD * NROW):
                            maxima(quad, m, k % 2)
                        if k == 2 * (NROW - LEAD) - 1 and not (last and s == QUAD - 1):
                            split(quad * QUAD + (s + 1), (s + 1) % 2)

            for m in range(NROW + LEAD):
                for j in range(2):
                    maxima(0, m, j)
                if m == NROW - 1:
                    split(0, 0)
            quad_steps(0, first=True)
            with dve.Fori(1, NQUAD - 1) as quad:
                quad_steps(quad)
            quad_steps(NQUAD - 1, last=True)

        @block.scalar
        def _(act):
            for i in range(2):
                act.sem_inc(mixed_stored[i], 16)
                act.sem_inc(denom_stored[i], 16)

            def exponents(quad, s, st, h):
                n = (s * ST + st) * G + h
                before, old = tile_before(s, st)
                if h == 0 and not (isinstance(quad, int) and quad == 0 and before < 0):
                    act.wait_ge(mix_done, quad * (QUAD * ST) + (before * ST + old + 1 + MIX0))
                    if old in POOL:
                        act.wait_ge(pool_added, quad * (QUAD * NPOOL) + (before * NPOOL + max(POOL.index(old), 1)))
                act.wait_ge(logit_done, quad * (QUAD * ST * G) + (n + 1 + LOGITS0))
                w = min(P, S - st * P)
                nc.scalar.activation(weights[buffer(s, st)][0:w, h, :], logit[h % 2][0:w, :], ACT.Exp).then_inc(exp_done, 1)

            def copy_parts(step, before, uses):
                act.wait_ge(turn_done, step + 1)
                if before is not None:
                    act.wait_ge(shift_in[before], uses)
                nc.scalar.copy(parts_t[:], logit[0][0:3 * NROW, 0:P]).then_inc(turn_copied, 1)

            def copy_mixed(quad, s):
                act.wait_ge(mix_done, quad * (QUAD * ST) + ((s + 1) * ST + MIX0))
                act.wait_ge(mixed_stored[s % 2], quad * 32 + (16 * (s // 2) + 16))
                nc.scalar.copy(mixed_sb[s % 2][:], mixed[:]).then_inc(mixed_copied, 1)

            def copy_denominators(quad, s):
                act.wait_ge(denom_done, quad * QUAD + (s + 3))
                act.wait_ge(denom_stored[s % 2], quad * 32 + (16 * (s // 2) + 16))
                nc.scalar.copy(denom_sb[s % 2][:], denom[:]).then_inc(denom_copied, 1)

            def quad_steps(quad, first=False, last=False):
                for s in range(QUAD):
                    for st in range(ST):
                        for h in range(G):
                            exponents(quad, s, st, h)
                            if h == 0 and not (first and s == 0):
                                if st == MIXED_AT:
                                    copy_mixed(quad, s - 1)
                                if st == DENOM_AT:
                                    copy_denominators(quad, s - 1)
                        if st == TURN_AT and not (last and s == QUAD - 1):
                            copy_parts(quad * QUAD + (s + 1), s, quad * 48 + 48)

            copy_parts(0, None, 0)
            quad_steps(0, first=True)
            with act.Fori(1, NQUAD - 1) as quad:
                quad_steps(quad)
            quad_steps(NQUAD - 1, last=True)
            copy_mixed(NQUAD - 1, QUAD - 1)
            copy_denominators(NQUAD - 1, QUAD - 1)


def output(nc, x_flat, wo, bo, gamma, beta, a_dram, d_dram, r_dram, out_flat):
    NT = OQ // P
    NOB = B * L // OQ
    with ExitStack() as held:
        def sb(name, shape, dt=F32):
            return held.enter_context(nc.sbuf_tensor(name, shape, dt))

        def sem(name):
            return held.enter_context(nc.semaphore(name))

        wo_raw = sb("wo_raw", [P, KVH, H])
        wo_hi, wo_lo = sb("wo_hi", [P, KVH, H], F32R), sb("wo_lo", [P, KVH, H], F32R)
        bo_row, gamma_row, beta_row = sb("bo_row", [P, H]), sb("gamma_row", [P, H]), sb("beta_row", [P, H])
        a_in = [sb(f"a_in{i}", [P, KVH, OQ]) for i in range(2)]
        r_in = [sb(f"r_in{i}", [P, KVH, OQ]) for i in range(2)]
        dens = sb("dens", [P, NSTEP * G * LQ // P])
        a_hi = [sb(f"a_hi{i}", [P, KVH, OQ], F32R) for i in range(2)]
        a_lo = [sb(f"a_lo{i}", [P, KVH, OQ], F32R) for i in range(2)]
        resid = [sb(f"resid{i}", [P, H]) for i in range(NT)]
        total = [sb(f"total{i}", [P, H]) for i in range(NT)]
        stats = [sb(f"stats{i}", [P, 2, 6]) for i in range(NT)]
        moments = [sb(f"moments{i}", [P, 2]) for i in range(NT)]
        spread = [sb(f"spread{i}", [P, 2]) for i in range(NT)]
        eps = sb("eps", [P, 1])
        acc = [held.enter_context(nc.psum_tensor(f"acc{i}", [P, 2, 512], F32)) for i in range(NT)]

        w_in, rows_in = sem("wo_in"), sem("rows_const_in")
        w_hi_done, w_lo_done = sem("wo_hi_done"), sem("wo_lo_done")
        eps_done = sem("eps_done")
        dens_in, dens_recip, dens_out = sem("dens_in"), sem("dens_recip"), sem("dens_out")
        a_landed = [sem(f"a_landed{i}") for i in range(2)]
        normed_done = sem("normed_done")
        a_hi_done, a_lo_done = sem("a_hi_done"), sem("a_lo_done")
        x_landed = [sem(f"x_landed{i}") for i in range(NT)]
        resid_done = sem("resid_done")
        proj_done = sem("proj_done")
        total_done = sem("total_done")
        chain = sem("chain")
        stats_seen = sem("stats_seen")
        std_done = sem("std_done")
        recip_done = sem("std_recip_done")
        scaled = sem("scaled")
        final = sem("final")
        stored = sem("out_stored")
        free = [sem(f"total_free{i}") for i in range(NT)]

        block = held.enter_context(nc.Block())

        @block.sync
        def _(sp):
            sp.dma_start(dens[:], d_dram.rearrange("a h l -> (a h l)").rearrange("(p n) -> p n", p=P)).then_inc(dens_in, 16)
            sp.dma_start(wo_raw[:], wo.rearrange("(t p) n -> p t n", p=P)).then_inc(w_in, 16)
            for row, src in ((bo_row, bo), (gamma_row, gamma), (beta_row, beta)):
                sp.dma_start(row[:], src.partition_broadcast(P)).then_inc(rows_in, 16)
            sp.wait_ge(dens_recip, 1)
            sp.dma_start(r_dram.rearrange("a h l -> (a h l)").rearrange("(p n) -> p n", p=P), dens[:]).then_inc(dens_out, 16)
            sp.wait_ge(dens_out, 16)

            def load_block(i, j):
                sp.wait_ge(a_lo_done, i * 2 + (j + 1))
                cols = slice(j * OQ, (j + 1) * OQ)
                sp.dma_start(a_in[j][:], a_dram[bass.ds(i * KVH, KVH), :, cols].rearrange("k p l -> p k l")).then_inc(a_landed[j], 16)
                for h in range(G):
                    sp.dma_start(r_in[j][h * HD:(h + 1) * HD], r_dram[bass.ds(i * KVH, KVH), h, cols].partition_broadcast(HD)).then_inc(a_landed[j], 16)

            def load_x(i, j):
                for t in range(NT):
                    sp.wait_ge(total_done, i * (2 * NT) + (j * NT + t + 1))
                    sp.dma_start(resid[t][:], x_flat[bass.ds(i * (2 * OQ) + (j * OQ + t * P), P), :]).then_inc(x_landed[t], 16)

            for j in range(2):
                load_block(0, j)
            with sp.Fori(0, NOB // 2 - 1) as i:
                for j in range(2):
                    load_x(i, j)
                    load_block(i + 1, j)
            for j in range(2):
                load_x(NOB // 2 - 1, j)

        @block.tensor
        def _(pe):
            pe.sem_inc(proj_done, 2 * NT)
            pe.wait_ge(w_lo_done, KVH)
            with pe.Fori(0, NOB // 2) as i:
                for j in range(2):
                    pe.wait_ge(a_lo_done, i * 2 + (j + 3))
                    for t in range(NT):
                        pe.wait_ge(total_done, i * (2 * NT) + (j * NT + t + 1))
                        cols = slice(t * P, (t + 1) * P)
                        for n in range(2):
                            out_cols = slice(n * 512, (n + 1) * 512)
                            terms = [(a, w, k) for a, w in ((a_hi[j], wo_hi), (a_lo[j], wo_hi), (a_hi[j], wo_lo)) for k in range(KVH)]
                            for m, (a, w, k) in enumerate(terms):
                                last = nc.tensor.matmul(acc[t][:, n, :], a[:, k, cols], w[:, k, out_cols], start=(m == 0), stop=(m == len(terms) - 1))
                        last.then_inc(proj_done, 1)

        @block.scalar
        def _(act):
            act.wait_ge(w_in, 16)
            for k in range(KVH):
                nc.scalar.copy(wo_hi[:, k, :], wo_raw[:, k, :]).then_inc(w_hi_done, 1)
            act.wait_ge(eps_done, 1)
            def split_hi(pair, j):
                act.wait_ge(normed_done, pair * 2 + (j + 1))
                act.wait_ge(proj_done, (pair * 2 + j) * NT + NT)
                nc.scalar.copy(a_hi[j][:], a_in[j][:]).then_inc(a_hi_done, 1)

            def deviations(pair, j):
                for t in range(NT):
                    act.wait_ge(chain, ((pair * 2 + j) * NT + (t + 1)) * 3)
                    nc.scalar.activation(spread[t][:, 0:1], moments[t][:, 1:2], ACT.Sqrt, bias=eps[:]).then_inc(std_done, 1)

            split_hi(0, 0)
            with act.Fori(0, NOB // 2 - 1) as i:
                split_hi(i, 1)
                deviations(i, 0)
                split_hi(i + 1, 0)
                deviations(i, 1)
            split_hi(NOB // 2 - 1, 1)
            deviations(NOB // 2 - 1, 0)
            deviations(NOB // 2 - 1, 1)

        @block.vector
        def _(dve):
            dve.sem_inc(a_lo_done, 2)
            dve.sem_inc(total_done, NT)
            dve.wait_ge(dens_in, 16)
            nc.vector.reciprocal(dens[:], dens[:]).then_inc(dens_recip, 1)
            for k in range(KVH):
                dve.wait_ge(w_hi_done, k + 1)
                nc.vector.tensor_tensor(wo_lo[:, k, :], wo_raw[:, k, :], wo_hi[:, k, :].bitcast(F32), ALU.subtract).then_inc(w_lo_done, 1)
            def normalise(i, j):
                dve.wait_ge(a_landed[j], i * (16 + 16 * G) + (16 + 16 * G))
                nc.vector.tensor_tensor(a_in[j][:], a_in[j][:], r_in[j][:], ALU.mult).then_inc(normed_done, 1)

            def split_lo(i, j):
                dve.wait_ge(a_hi_done, i * 2 + (j + 1))
                nc.vector.tensor_tensor(a_lo[j][:], a_in[j][:], a_hi[j][:].bitcast(F32), ALU.subtract).then_inc(a_lo_done, 1)

            def norm(i, j):
                for t in range(NT):
                    n = i * (2 * NT) + (j * NT + t)
                    dve.wait_ge(proj_done, n + (2 * NT + 1))
                    dve.wait_ge(resid_done, n + 1)
                    dve.wait_ge(free[t], i * 2 + (j + 1))
                    nc.vector.tensor_tensor(total[t][:].rearrange("p (c n) -> p c n", c=2), acc[t][:], resid[t][:].rearrange("p (c n) -> p c n", c=2), ALU.add).then_inc(total_done, 1)
                    dve.wait_ge(total_done, n + (NT + 1))
                    for c in range(2):
                        nc.vector.bn_stats(stats[t][:, c, :], total[t][:, c * 512:(c + 1) * 512]).then_inc(chain, 1)
                    dve.wait_ge(chain, n * 3 + 2)
                    dve.sem_inc(stats_seen, 1)
                    nc.vector.bn_aggr(moments[t][:], stats[t][:].rearrange("p c s -> p (c s)")).then_inc(chain, 1)
                    dve.wait_ge(std_done, n + 1)
                    nc.vector.reciprocal(spread[t][:, 1:2], spread[t][:, 0:1]).then_inc(recip_done, 1)
                    dve.wait_ge(recip_done, n + 1)
                    nc.vector.tensor_scalar(total[t][:], total[t][:], moments[t][:, 0:1], spread[t][:, 1:2], ALU.subtract, ALU.mult).then_inc(scaled, 1)
                    dve.wait_ge(scaled, n * 2 + 1)
                    nc.vector.tensor_tensor(total[t][:], total[t][:], gamma_row[:], ALU.mult).then_inc(scaled, 1)

            normalise(0, 0)
            normalise(0, 1)
            split_lo(0, 0)
            with dve.Fori(0, NOB // 2 - 1) as i:
                split_lo(i, 1)
                normalise(i + 1, 0)
                norm(i, 0)
                split_lo(i + 1, 0)
                normalise(i + 1, 1)
                norm(i, 1)
            split_lo(NOB // 2 - 1, 1)
            norm(NOB // 2 - 1, 0)
            norm(NOB // 2 - 1, 1)

        @block.gpsimd
        def _(pool):
            nc.gpsimd.memset(eps[:], EPS).then_inc(eps_done, 1)
            for t in range(NT):
                pool.sem_inc(free[t], 1)
            pool.wait_ge(rows_in, 48)

            def add_bias(i, j, t):
                pool.wait_ge(x_landed[t], i * 32 + (j * 16 + 16))
                nc.gpsimd.tensor_tensor(resid[t][:], resid[t][:], bo_row[:], ALU.add).then_inc(resid_done, 1)

            with pool.Fori(0, NOB // 2) as i:
                for j in range(2):
                    for t in range(NT):
                        add_bias(i, j, t)
                    for t in range(NT):
                        n = i * (2 * NT) + (j * NT + t)
                        pool.wait_ge(scaled, n * 2 + 2)
                        nc.gpsimd.tensor_tensor(total[t][:], total[t][:], beta_row[:], ALU.add).then_inc(final, 1)
                        pool.wait_ge(final, n + 1)
                        pool.dma_start(out_flat[bass.ds(i * (2 * OQ) + (j * OQ + t * P), P), :], total[t][:]).then_inc(stored, 16)
                        pool.wait_ge(stored, n * 16 + 16)
                        pool.sem_inc(free[t], 1)


_INS = ["x", "ctx_2048", "mask_Bx1xSxS2_ff0"] + ["L0_xattn_" + n for n in ("Wq", "bq", "Wk", "bk", "Wv", "bv", "Wo", "bo", "gamma", "beta")]


def kernel(**inputs):
    import concourse.bacc as bacc
    from concourse.bass_utils import run_bass_kernel_spmd

    nc = bacc.Bacc("TRN2", target_bir_lowering=False, num_devices=1)
    arrays, args = {}, []
    for name in _INS:
        a = np.ascontiguousarray(inputs[name])
        arrays[f"in_{name}"] = a
        args.append(nc.dram_tensor(f"in_{name}", a.shape, mybir.dt.from_np(a.dtype), kind="ExternalInput").ap())
    out = nc.dram_tensor("out", (B, L, H), F32, kind="ExternalOutput").ap()
    xattn_program(nc, *args, out)
    r = run_bass_kernel_spmd(nc, [arrays], core_ids=[0])
    return r.results[0]["out"]
```

```python
from contextlib import ExitStack

import numpy as np

import concourse.bass as bass
from concourse import mybir

F32 = mybir.dt.float32
F32R = mybir.dt.float32r
ALU = mybir.AluOpType
ACT = mybir.ActivationFunctionType

P = 128
B, L, H = 4, 1024, 1024
S = 1601
NH, KVH, HD = 32, 8, 32
G = NH // KVH
KV = KVH * HD
KT = H // P
SCALE = float(HD) ** -0.5
EPS = 1e-6

XC = 512
NXC = B * L // XC
NCC = -(-B * S // XC)
LQ = 512
NLQ = B * L // LQ
NSTEP = NLQ * KVH
ST = -(-S // P)
SLAST = S - (ST - 1) * P
STACK = 3 * HD
SHIFT = STACK + 3
OQ = 256
MT = B * L // P
EARLY = 3
FMAX = 3.0e38
FAR = 1.0e37
SPAD = 1604
HALVES = ((0, 400, 400), (800, 1202, 402))


def xattn_program(nc, x, ctx_kv, mask, wq, bq, wk, bk, wv, bv, wo, bo, gamma, beta, out):
    x_flat = x.rearrange("b l h -> (b l) h")
    ctx_flat = ctx_kv.rearrange("b s h -> (b s) h")
    mask_flat = mask.rearrange("b o l s -> (b o l) s")
    out_flat = out.rearrange("b l h -> (b l) h")

    q_dram = nc.dram_tensor("q_parts", [NLQ, KVH, 2, P, LQ], F32, kind="Internal").ap()
    k_dram = nc.dram_tensor("k_parts", [2, KV, B * S], F32, kind="Internal").ap()
    v_dram = nc.dram_tensor("v_rows", [B * S, KV], F32, kind="Internal").ap()
    a_dram = nc.dram_tensor("weighted", [NSTEP, P, LQ], F32, kind="Internal").ap()
    d_dram = nc.dram_tensor("denominators", [NSTEP, G, LQ], F32, kind="Internal").ap()
    r_dram = nc.dram_tensor("reciprocals", [NSTEP, G, LQ], F32, kind="Internal").ap()

    with ExitStack() as whole:
        ident = whole.enter_context(nc.sbuf_tensor("ident", [P, P], F32))
        mask_size = whole.enter_context(nc.sbuf_tensor("mask_size", [P, MT], F32))
        project(nc, x_flat, ctx_flat, mask_flat, wq, bq, wk, bk, wv, bv, q_dram, k_dram, v_dram, ident, mask_size)
        wo_early = whole.enter_context(nc.sbuf_tensor("wo_early", [P, EARLY, H], F32))
        attend(nc, mask_flat, q_dram, k_dram, v_dram, a_dram, d_dram, ident, mask_size, wo, wo_early)
        output(nc, x_flat, wo, wo_early, bo, gamma, beta, a_dram, d_dram, r_dram, out_flat)


def project(nc, x_flat, ctx_flat, mask_flat, wq, bq, wk, bk, wv, bv, q_dram, k_dram, v_dram, ident, mask_size):
    XG, KG = KT, KV // P
    CG = KG + XC // P
    BESIDE = {"x": [(t,) for t in range(KT)], "ctx": [(0, 1), (2, 3), (4,), (5,), (6,), (7,)]}
    HALF = H // 2
    MPC = MT // NXC

    def chunk(kind, c):
        return c if kind == "ctx" else c + NCC

    def sums(kind, c):
        return c * CG if kind == "ctx" else c * XG + NCC * CG

    def parts(kind, c):
        return c * KG if kind == "ctx" else c * XG + NCC * KG

    def start(c):
        return B * S - XC if isinstance(c, int) and c == NCC - 1 else c * XC

    def bank(kind, par, g):
        return ((par * CG if kind == "ctx" else NCC * CG) + g) % 4

    def final(kind, c):
        return kind == "x" and isinstance(c, int) and c == NXC - 1

    def all_chunks(engine, step):
        with engine.Fori(0, NCC // 2 - 1) as i:
            for par in range(2):
                step("ctx", i * 2 + par, par)
        for c in range(NCC - 3, NCC):
            step("ctx", c, c % 2)
        with engine.Fori(0, NXC // 2 - 1) as i:
            for par in range(2):
                step("x", i * 2 + par, (par + NCC) % 2)
        for c in range(NXC - 2, NXC):
            step("x", c, (c + NCC) % 2)

    with ExitStack() as held:
        def sb(name, shape, dt=F32):
            return held.enter_context(nc.sbuf_tensor(name, shape, dt))

        def sem(name):
            return held.enter_context(nc.semaphore(name))

        wq_hi, wq_lo = sb("wq_hi", [P, KT, H], F32R), sb("wq_lo", [P, KT, H], F32R)
        wk_hi, wk_lo = sb("wk_hi", [P, KT, KV], F32R), sb("wk_lo", [P, KT, KV], F32R)
        wv_hi, wv_lo = sb("wv_hi", [P, KT, KV], F32R), sb("wv_lo", [P, KT, KV], F32R)
        bq_col, bk_col = sb("bq_col", [P, KT]), sb("bk_col", [P, KG])
        bq_scaled = sb("bq_scaled", [P, KT])
        bv_row = sb("bv_row", [P, KV])
        rows = sb("rows", [P, XC // P, H])
        t_hi = [sb(f"t_hi{i}", [P, KT, XC], F32R) for i in range(2)]
        t_lo = [sb(f"t_lo{i}", [P, KT, XC], F32R) for i in range(2)]
        full = [sb(f"full{i}", [P, XC]) for i in range(2)]
        o_hi = [sb(f"o_hi{i}", [P, XC], F32R) for i in range(2)]
        o_lo = [sb(f"o_lo{i}", [P, XC], F32R) for i in range(2)]
        v_out = [sb(f"v_out{i}", [P, KV]) for i in range(2)]
        landing = sb("landing", [P, 2 * S])
        LAND = 2 * S // H
        turned = [held.enter_context(nc.psum_tensor(f"turned{i}", [P, XC], F32)) for i in range(2)]
        summed = [held.enter_context(nc.psum_tensor(f"summed{i}", [P, XC], F32)) for i in range(4)]

        w_pieces = [(w.rearrange("(t p) n -> p t n", p=P)[:, t:t + n], hi[:, t:t + n, :], lo[:, t:t + n, :])
                    for w, hi, lo, n in ((wk, wk_hi, wk_lo, H // KV), (wv, wv_hi, wv_lo, H // KV), (wq, wq_hi, wq_lo, 1))
                    for t in range(0, KT, n)]
        KVW = 2 * KT * KV // H
        W_RUNS = (range(KVW), range(KVW, KVW + 3), range(KVW + 3, KVW + 6), range(KVW + 6, len(w_pieces)))
        w_in = [sem(f"w_in{i}") for i in range(LAND)]
        w_hi_done, w_lo_done = sem("w_hi_done"), sem("w_lo_done")
        bias_in = sem("bias_in")
        bias_done = sem("bias_done")
        ident_zero, ident_done = sem("ident_zero"), sem("ident_done")
        rows_in = [sem(f"rows_in{i}") for i in range(2)]
        turn_done = sem("turn_done")
        hi_done = sem("hi_done")
        lo_done = sem("lo_done")
        sum_done = sem("sum_done")
        sum_read = sem("sum_read")
        part_hi = sem("part_hi")
        part_lo = sem("part_lo")
        part_stored = sem("part_stored")
        v_stored = sem("v_stored")
        mask_in = [sem(f"mask_tile_in{i}") for i in range(2)]
        mask_sized = sem("mask_sized")
        mask_seen = sem("mask_seen")
        part_free = [sem(f"part_free{i}") for i in range(2)]
        v_free = [sem(f"v_free{i}") for i in range(2)]

        block = held.enter_context(nc.Block())

        @block.sync
        def _(sp):
            def load(kind, c, half):
                u = chunk(kind, c)
                if not (isinstance(u, int) and u == 0):
                    sp.wait_ge(turn_done, u * KT + (half - 1) * KT // 2)
                src, first = (ctx_flat, start(c)) if kind == "ctx" else (x_flat, c * XC)
                cols = slice(half * HALF, (half + 1) * HALF)
                sp.dma_start(rows[:, :, cols], src[bass.ds(first, XC), cols].rearrange("(t p) h -> p t h", p=P)).then_inc(rows_in[half], 16)

            def load_mask(c, j):
                tile = c * MPC + j
                sp.wait_ge(mask_sized, tile + 1)
                sp.dma_start(landing[:, j % 2 * S:(j % 2 + 1) * S], mask_flat[bass.ds(tile * P, P), :]).then_inc(mask_in[j % 2], 16)

            def step(kind, c, par):
                turns = kind == "ctx" and isinstance(c, int) and c == NCC - 1
                following = ("x", 0) if turns else (kind, c + 1)
                for half in range(2):
                    if not final(kind, c):
                        load(*following, half)
                if kind == "x":
                    for j in range(MPC):
                        load_mask(c, j)
                if turns:
                    sp.wait_ge(w_lo_done, len(w_pieces))

            for half in range(2):
                load("ctx", 0, half)
            with nc.allow_non_contiguous_dma(reason="biases by column"):
                sp.dma_start(bq_col[:], bq.rearrange("(c p) -> p c", p=P)).then_inc(bias_in, 16)
                sp.dma_start(bk_col[:], bk.rearrange("(c p) -> p c", p=P)).then_inc(bias_in, 16)
            sp.dma_start(bv_row[:], bv.partition_broadcast(P)).then_inc(bias_in, 16)
            all_chunks(sp, step)

        @block.tensor
        def _(pe):
            pe.sem_inc(sum_done, 1)
            pe.wait_ge(ident_done, 1)

            def turn(u, t):
                if t % (KT // 2) == 0:
                    pe.wait_ge(rows_in[t // (KT // 2)], u * 16 + 16)
                pe.wait_ge(lo_done, u * KT + (t + 1))
                for a in range(XC // P):
                    last = nc.tensor.transpose(turned[t % 2][:, a * P:(a + 1) * P], rows[:, a, t * P:(t + 1) * P], ident[:])
                last.then_inc(turn_done, 1)

            def three(acc, pairs):
                for n, (lhs, rhs) in enumerate(pairs):
                    last = nc.tensor.matmul(acc, lhs, rhs, start=(n == 0), stop=(n == len(pairs) - 1))
                last.then_inc(sum_done, 1)

            def step(kind, c, par):
                u = chunk(kind, c)
                hi, lo = t_hi[par], t_lo[par]
                for g, beside in enumerate(BESIDE[kind]):
                    if not final(kind, c):
                        for t in beside:
                            turn(u + 1, t)
                    if g == 0:
                        pe.wait_ge(lo_done, u * KT + (KT + 2))
                    pe.wait_ge(sum_read, sums(kind, c) + (g + 1))
                    acc = summed[bank(kind, par, g)]
                    if kind == "x" or g < KG:
                        w_hi, w_lo = (wq_hi, wq_lo) if kind == "x" else (wk_hi, wk_lo)
                        cols = slice(g * P, (g + 1) * P)
                        three(acc[:], [(w[:, t, cols], m[:, t, :]) for w, m in ((w_hi, hi), (w_hi, lo), (w_lo, hi)) for t in range(KT)])
                    else:
                        cols = slice((g - KG) * P, (g - KG + 1) * P)
                        three(acc[:, 0:KV], [(m[:, t, cols], w[:, t, :]) for m, w in ((hi, wv_hi), (lo, wv_hi), (hi, wv_lo)) for t in range(KT)])

            for t in range(KT):
                turn(0, t)
            pe.wait_ge(w_lo_done, KVW)
            with pe.Fori(0, NCC // 2 - 1) as i:
                for par in range(2):
                    step("ctx", i * 2 + par, par)
            for c in range(NCC - 3, NCC):
                step("ctx", c, c % 2)
            pe.wait_ge(w_lo_done, len(w_pieces))
            with pe.Fori(0, NXC // 2 - 1) as i:
                for par in range(2):
                    step("x", i * 2 + par, (par + NCC) % 2)
            for c in range(NXC - 2, NXC):
                step("x", c, (c + NCC) % 2)

        @block.scalar
        def _(act):
            def landed(n):
                hi = w_pieces[n][1]
                return landing[:, n % LAND * H:(n % LAND + 1) * H].rearrange("p (t n) -> p t n", t=hi.shape[1])

            def load_weights(pieces):
                for n in pieces:
                    if n >= LAND:
                        act.wait_ge(w_lo_done, n - LAND + 1)
                    act.dma_start(landed(n), w_pieces[n][0]).then_inc(w_in[n % LAND], 16)

            def split_weights_hi(pieces):
                for n in pieces:
                    act.wait_ge(w_in[n % LAND], n // LAND * 16 + 16)
                    nc.scalar.copy(w_pieces[n][1], landed(n)).then_inc(w_hi_done, 1)

            load_weights(range(LAND))

            def split_hi(u, t, par):
                act.wait_ge(turn_done, u * KT + (t + 1))
                nc.scalar.copy(t_hi[par][:, t, :], turned[t % 2][:]).then_inc(hi_done, 1)

            def step(kind, c, par):
                u, n0 = chunk(kind, c), sums(kind, c)
                act.wait_ge(sum_done, n0 + 1)
                for g, beside in enumerate(BESIDE[kind]):
                    if not final(kind, c):
                        for t in beside:
                            split_hi(u + 1, t, 1 - par)
                    if kind == "ctx" and isinstance(c, int) and g == 2:
                        split_weights_hi(W_RUNS[c - NCC + 4])
                    if kind == "x" or g < KG:
                        act.wait_ge(sum_done, n0 + (g + 2))
                        act.wait_ge(part_free[g % 2], c + 1 if kind == "ctx" else c * (XG // 2) + (NCC + g // 2 + 1))
                        acc = summed[bank(kind, par, g)][:]
                        if kind == "x":
                            ins = nc.scalar.activation(o_hi[g % 2][:], acc, ACT.Identity, bias=bq_scaled[:, g:g + 1], scale=SCALE)
                        else:
                            ins = nc.scalar.activation(o_hi[g % 2][:], acc, ACT.Identity, bias=bk_col[:, g:g + 1])
                        ins.then_inc(part_hi, 1)
                if kind == "ctx" and isinstance(c, int) and c < NCC - 1:
                    load_weights(W_RUNS[c - NCC + 5])

            for t in range(KT):
                split_hi(0, t, 0)
            split_weights_hi(range(KVW - LAND))
            load_weights(range(LAND, KVW))
            split_weights_hi(range(KVW - LAND, KVW))
            load_weights(W_RUNS[1])
            act.wait_ge(bias_in, 48)
            act.wait_ge(bias_done, 1)
            all_chunks(act, step)

        @block.vector
        def _(dve):
            dve.sem_inc(lo_done, 2)
            dve.sem_inc(sum_read, 4)
            dve.sem_inc(mask_sized, 2)

            def split_lo(u, t, par):
                dve.wait_ge(hi_done, u * KT + (t + 1))
                nc.vector.tensor_tensor(t_lo[par][:, t, :], turned[t % 2][:], t_hi[par][:, t, :].bitcast(F32), ALU.subtract).then_inc(lo_done, 1)

            def split_weights_lo(pieces):
                for n in pieces:
                    _, hi, lo = w_pieces[n]
                    dve.wait_ge(w_hi_done, n + 1)
                    raw = landing[:, n % LAND * H:(n % LAND + 1) * H].rearrange("p (t n) -> p t n", t=hi.shape[1])
                    nc.vector.tensor_tensor(lo, raw, hi.bitcast(F32), ALU.subtract).then_inc(w_lo_done, 1)

            def look_through(c, j):
                dve.wait_ge(mask_in[j % 2], c * (8 * MPC) + (j // 2 + 1) * 16)
                dve.sem_inc(mask_seen, 1)
                nc.vector.tensor_reduce(mask_size[:, bass.ds(c * MPC + j, 1)], landing[:, j % 2 * S:(j % 2 + 1) * S], mybir.AxisListType.X, ALU.max,
                                        apply_absolute_value=True).then_inc(mask_sized, 1)

            def step(kind, c, par):
                u, n0 = chunk(kind, c), sums(kind, c)
                for g, beside in enumerate(BESIDE[kind]):
                    if not final(kind, c):
                        for t in beside:
                            split_lo(u + 1, t, 1 - par)
                    if kind == "ctx" and isinstance(c, int) and g == 2:
                        split_weights_lo(W_RUNS[c - NCC + 4])
                    acc = summed[bank(kind, par, g)]
                    if kind == "x" or g < KG:
                        dve.wait_ge(part_hi, parts(kind, c) + (g + 1))
                        if kind == "x":
                            ins = nc.vector.tensor_scalar(full[g % 2][:], acc[:], SCALE, bq_scaled[:, g:g + 1], ALU.mult, ALU.add)
                        else:
                            ins = nc.vector.tensor_scalar(full[g % 2][:], acc[:], bk_col[:, g:g + 1], None, ALU.add)
                        ins.then_inc(sum_read, 1)
                        dve.wait_ge(sum_read, n0 + (g + 5))
                        nc.vector.tensor_tensor(o_lo[g % 2][:], full[g % 2][:], o_hi[g % 2][:].bitcast(F32), ALU.subtract).then_inc(part_lo, 1)
                    else:
                        j = g - KG
                        dve.wait_ge(sum_done, n0 + (g + 2))
                        dve.wait_ge(v_free[j % 2], c * (XC // P // 2) + (j // 2 + 1))
                        nc.vector.tensor_tensor(v_out[j % 2][:], acc[:, 0:KV], bv_row[:], ALU.add).then_inc(sum_read, 1)
                    if kind == "x" and g % 2:
                        look_through(c, g // 2)

            for t in range(KT):
                split_lo(0, t, 0)
            split_weights_lo(W_RUNS[0])
            dve.wait_ge(bias_in, 48)
            nc.vector.tensor_scalar(bq_scaled[:], bq_col[:], SCALE, None, ALU.mult).then_inc(bias_done, 1)
            dve.wait_ge(bias_done, 1)
            all_chunks(dve, step)
            dve.wait_ge(mask_sized, 2 + MT)

        @block.gpsimd
        def _(pool):
            nc.gpsimd.memset(ident[:], 0.0).then_inc(ident_zero, 1)
            pool.wait_ge(ident_zero, 1)
            nc.gpsimd.affine_select(out=ident[:], in_=ident[:], compare_op=ALU.not_equal, fill=1.0, base=0,
                                    pattern=[[-1, P]], channel_multiplier=1).then_inc(ident_done, 1)
            for i in range(2):
                pool.sem_inc(part_free[i], 1)
                pool.sem_inc(v_free[i], 1)

            def step(kind, c, par):
                p0 = parts(kind, c)
                for g in range(XG if kind == "x" else KG):
                    pool.wait_ge(part_lo, p0 + (g + 1))
                    for n, part in enumerate((o_hi, o_lo)):
                        if kind == "x":
                            dst = q_dram[bass.ds(c, 1), g, n].rearrange("a p l -> (a p) l")
                        else:
                            dst = k_dram[n, g * P:(g + 1) * P, bass.ds(start(c), XC)]
                        pool.dma_start(dst, part[g % 2][:].bitcast(F32)).then_inc(part_stored, 16)
                    pool.wait_ge(part_stored, p0 * 32 + 32 * (g + 1))
                    pool.sem_inc(part_free[g % 2], 1)
                if kind == "ctx":
                    for j in range(XC // P):
                        pool.wait_ge(sum_read, sums(kind, c) + (KG + j + 1 + 4))
                        pool.dma_start(v_dram[bass.ds(start(c) + j * P, P), :], v_out[j % 2][:]).then_inc(v_stored, 16)
                        pool.wait_ge(v_stored, c * (16 * XC // P) + 16 * (j + 1))
                        pool.sem_inc(v_free[j % 2], 1)

            all_chunks(pool, step)


def attend(nc, mask_flat, q_dram, k_dram, v_dram, a_dram, d_dram, ident, mask_size, wo, wo_early):
    QUAD = 4
    NQUAD = NSTEP // QUAD
    NROW = G * LQ // P
    LEAD = 6
    LAG = 2
    POOL = (0, 1, 3, 4, 6, 7, 8, 9, 10)
    REST = tuple(st for st in range(ST) if st not in POOL)
    RINGS = (4, 2)
    SUMS_AT = 2
    DENSE = [st == SUMS_AT or (st - LAG) % ST in REST for st in range(ST)]
    PACE = [(1, 1, 0, 1) if DENSE[st] else (1, int(st == 9), 1, 0) for st in range(ST)]
    assert sum(map(sum, PACE)) == 2 * NROW
    assert DENSE[LAG] and DENSE[(ST - 1 + LAG) % ST]
    MIXED_AT, DENOM_AT = 2, 3
    TURN_AT = 10
    NPOOL = len(POOL) - 1
    QB = 4
    NLT = LQ // P
    NB = L // LQ

    def ring(st):
        return (POOL, RINGS[0], 0) if st in POOL else (REST, RINGS[1], RINGS[0])

    def buffer(s, st):
        tiles, size, first = ring(st)
        return first + (s * len(tiles) + tiles.index(st)) % size

    def tile_before(s, st):
        tiles, size, _ = ring(st)
        n = s * len(tiles) + tiles.index(st) - size
        return n // len(tiles), tiles[n % len(tiles)]

    with ExitStack() as held:
        def sb(name, shape, dt=F32):
            return held.enter_context(nc.sbuf_tensor(name, shape, dt))

        def sem(name):
            return held.enter_context(nc.semaphore(name))

        q_sb = [sb(f"q_sb{i}", [SHIFT, G, LQ], F32R) for i in range(QB)]
        k_sb = [sb(f"k_sb{i}", [SHIFT, SPAD], F32R) for i in range(QB)]
        v_sb = [sb(f"v_sb{i}", [P, ST, HD]) for i in range(QB)]
        mask_max = sb("mask_max", [P, NLT, SPAD])
        mask_exp = sb("mask_exp", [P, NLT, S])
        masked_row = [sb(f"masked_row{i}", [P, 2 * HALVES[i][2]]) for i in range(2)]
        half_max = sb("half_max", [P, 2])
        row_max = [sb(f"row_max{i}", [P, G, NLT]) for i in range(2)]
        rest = sb("rest", [P, NROW])
        parts = sb("parts", [P, 3, NROW], F32R)
        parts_t = sb("parts_t", [3 * NROW, P], F32R)
        weights = [sb(f"weights{i}", [P, G, LQ]) for i in range(sum(RINGS))]
        sum_pool = [sb(f"sum_pool{i}", [P, G, LQ]) for i in range(2)]
        ones = sb("ones", [P, HD])
        mixed_sb = [sb(f"mixed_sb{i}", [P, LQ]) for i in range(2)]
        denom_sb = [sb(f"denom_sb{i}", [P, LQ]) for i in range(2)]
        count = sb("count", [P, 1])
        flag = sb("flag", [1, 1], mybir.dt.int32)
        score = [held.enter_context(nc.psum_tensor(f"score{i}", [P, 2, 512], F32)) for i in range(2)]
        logit = [held.enter_context(nc.psum_tensor(f"logit{i}", [P, LQ], F32)) for i in range(2)]
        mixed = held.enter_context(nc.psum_tensor("mixed", [P, LQ], F32))
        denom = held.enter_context(nc.psum_tensor("denom", [P, LQ], F32))

        const_done = sem("const_done")
        count_done = sem("count_done")
        total_done = sem("count_total")
        flag_done = sem("flag_done")
        mask_in = [sem(f"mask_in{i}") for i in range(NLT)]
        mask_ready = [sem(f"mask_ready{i}") for i in range(NLT)]
        mask_exp_in = sem("mask_exp_in")
        mask_exp_seen = sem("mask_exp_seen")
        mask_exp_ready = sem("mask_exp_ready")
        qk_in = [sem(f"qk_in{i}") for i in range(QB)]
        v_in = [sem(f"v_in{i}") for i in range(QB)]
        score_done = sem("score_done")
        half_seen = sem("half_seen")
        max_done = sem("max_done")
        rest_done = sem("rest_done")
        parts_seen = sem("parts_seen")
        turn_done = sem("parts_turned")
        turn_copied = sem("turn_copied")
        shift_in = [sem(f"shift_in{i}") for i in range(QB)]
        logit_done = sem("logit_done")
        exp_done = sem("exp_done")
        pool_added = sem("pool_added")
        mix_done = sem("mix_done")
        mixed_copied = sem("mixed_copied")
        denom_done = sem("denom_done")
        denom_copied = sem("denom_copied")
        wo_in = sem("wo_early_in")
        sync_seen = sem("sync_seen")
        mixed_stored = [sem(f"mixed_stored{i}") for i in range(2)]
        denom_stored = [sem(f"denom_stored{i}") for i in range(2)]

        LOGITS0, MIX0, MAX0 = QB * ST * G, QB * ST, 2 * NROW

        block = held.enter_context(nc.Block())

        @block.sync
        def _(sp):
            sp.wait_ge(flag_done, 1)
            any_mask = sp.value_load(flag[0:1, 0:1], min_val=0, max_val=1)

            def load_step(b, lq, n):
                a, j = b * NB + lq, n % QB
                step = a * KVH + n
                sp.wait_ge(logit_done, step * (ST * G) + ST * G)
                sp.sem_inc(sync_seen, 1)
                for r, part in enumerate((0, 1, 0)):
                    src = q_dram[bass.ds(a, 1), n, part].rearrange("a (h d) l -> (a d) h l", d=HD)
                    sp.dma_start(q_sb[j][r * HD:(r + 1) * HD].bitcast(F32), src).then_inc(qk_in[j], 16)
                for r, part in enumerate((0, 0, 1)):
                    src = k_dram[part, n * HD:(n + 1) * HD, bass.ds(b * S, S)]
                    sp.dma_start(k_sb[j][r * HD:(r + 1) * HD, 0:S].bitcast(F32), src).then_inc(qk_in[j], 16)
                sp.wait_ge(mix_done, step * ST + ST)
                sp.sem_inc(sync_seen, 1)
                cols = slice(n * HD, (n + 1) * HD)
                sp.dma_start(v_sb[j][:, 0:ST - 1, :], v_dram[bass.ds(b * S, (ST - 1) * P), cols].rearrange("(t p) d -> p t d", p=P)).then_inc(v_in[j], 16)
                sp.dma_start(v_sb[j][0:SLAST, ST - 1, :], v_dram[bass.ds(b * S + (ST - 1) * P, SLAST), cols]).then_inc(v_in[j], 16)

            def load_mask(a, lt):
                sp.wait_ge(max_done, a * (2 * NROW * KVH) + 2 * G * (lt + 1))
                sp.sem_inc(sync_seen, 1)
                sp.dma_start(mask_max[:, lt, 0:S], mask_flat[bass.ds(a * LQ + lt * P, P), :]).then_inc(mask_in[lt], 16)

            def mask_landed(a, lt):
                sp.wait_ge(mask_in[lt], a * 16 + 16)
                sp.sem_inc(mask_ready[lt], KVH // QUAD)

            def load_mask_exp(a):
                with sp.If(any_mask > 0):
                    sp.wait_ge(logit_done, a * (KVH * ST * G) + LOGITS0)
                    sp.sem_inc(sync_seen, 1)
                    for lt in range(NLT):
                        sp.dma_start(mask_exp[:, lt, :], mask_flat[bass.ds(a * LQ + lt * P, P), :]).then_inc(mask_exp_in, 16)

            def shift(step, j):
                sp.wait_ge(turn_copied, step + 1)
                sp.sem_inc(sync_seen, 1)
                for r in range(3):
                    sp.dma_start(q_sb[j][STACK + r:STACK + r + 1].bitcast(F32).rearrange("a h (t l) -> a (h t) l", l=P),
                                 parts_t[r * NROW:(r + 1) * NROW, :].bitcast(F32)).then_inc(shift_in[j], 16)

            def store(step, par):
                sp.wait_ge(mixed_copied, step + 1)
                sp.sem_inc(sync_seen, 1)
                sp.dma_start(a_dram[bass.ds(step, 1)].rearrange("a p l -> (a p) l"), mixed_sb[par][:]).then_inc(mixed_stored[par], 16)
                sp.wait_ge(denom_copied, step + 1)
                sp.sem_inc(sync_seen, 1)
                sp.dma_start(d_dram[bass.ds(step, 1)].rearrange("a h l -> (a h) l"), denom_sb[par][0:P:HD, :]).then_inc(denom_stored[par], 16)

            def batch(b, first=False, last=False):
                for lq in range(NB):
                    for n in range(KVH):
                        a = b * NB + lq
                        step = a * KVH + n
                        if n == 0:
                            load_mask_exp(a)
                        ahead = lq * KVH + n + 3
                        if ahead < NB * KVH:
                            load_step(b, ahead // KVH, ahead % KVH)
                        elif not last:
                            load_step(b + 1, 0, ahead % KVH)
                        if not (first and lq == 0 and n == 0):
                            store(step - 1, (n - 1) % 2)
                        final = last and lq == NB - 1
                        if n == KVH - 2 and not final:
                            for lt in range(NLT - 1):
                                load_mask(a + 1, lt)
                            for lt in range(2):
                                mask_landed(a + 1, lt)
                            load_mask(a + 1, NLT - 1)
                        if not (final and n == KVH - 1):
                            shift(step + 1, (n + 1) % QB)
                        if n == KVH - 2 and not final:
                            for lt in range(2, NLT):
                                mask_landed(a + 1, lt)

            load_step(0, 0, 0)
            for lt in range(NLT):
                load_mask(0, lt)
            load_step(0, 0, 1)
            for lt in range(NLT):
                mask_landed(0, lt)
            load_step(0, 0, 2)
            shift(0, 0)
            sp.dma_start(wo_early[:], wo[0:EARLY * P].rearrange("(t p) n -> p t n", p=P)).then_inc(wo_in, 16)
            batch(0, first=True)
            with sp.Fori(1, B - 1) as b:
                batch(b)
            batch(B - 1, last=True)
            store(NSTEP - 1, 1)
            for i in range(2):
                sp.wait_ge(mixed_stored[i], 16 + 16 * (NSTEP // 2))
                sp.wait_ge(denom_stored[i], 16 + 16 * (NSTEP // 2))
            sp.wait_ge(wo_in, 16)

        @block.gpsimd
        def _(pool):
            nc.gpsimd.memset(mask_max[:, :, S:SPAD], -FMAX).then_inc(const_done, 1)
            pool.wait_ge(const_done, 1)
            nc.gpsimd.memset(ones[:], 1.0).then_inc(const_done, 1)
            for i, k in enumerate(k_sb):
                pool.wait_ge(const_done, 2 + 2 * i)
                nc.gpsimd.memset(k[0:STACK, S:SPAD].bitcast(F32), 0.0).then_inc(const_done, 1)
                pool.wait_ge(const_done, 3 + 2 * i)
                nc.gpsimd.memset(k[STACK:SHIFT, :].bitcast(F32), 1.0).then_inc(const_done, 1)

            def add(quad, s, n):
                step, st = quad * QUAD + s, POOL[n + 1]
                pool.wait_ge(exp_done, quad * (QUAD * ST * G) + (s * ST + st + 1) * G)
                if n == 0:
                    pool.wait_ge(denom_done, step + 1)
                    first = weights[buffer(s, POOL[0])]
                else:
                    pool.wait_ge(pool_added, step * NPOOL + n)
                    first = sum_pool[s % 2]
                nc.gpsimd.tensor_tensor(sum_pool[s % 2][:], first[:], weights[buffer(s, st)][:], ALU.add).then_inc(pool_added, 1)

            pool.wait_ge(flag_done, 1)
            any_mask = pool.value_load(flag[0:1, 0:1], min_val=0, max_val=1)
            with pool.Fori(0, NLQ) as a:
                with pool.If(any_mask > 0):
                    pool.wait_ge(mask_exp_in, a * (16 * NLT) + 16 * NLT)
                    pool.sem_inc(mask_exp_seen, 1)
                    nc.gpsimd.tensor_scalar(mask_exp[:], mask_exp[:], -FAR, None, ALU.max).then_inc(mask_exp_ready, KVH // QUAD)
                for q in range(KVH // QUAD):
                    for s in range(QUAD):
                        for n in range(NPOOL):
                            add(a * (KVH // QUAD) + q, s, n)

        @block.tensor
        def _(pe):
            pe.sem_inc(logit_done, LOGITS0)
            pe.sem_inc(mix_done, MIX0)
            pe.sem_inc(denom_done, 2)
            pe.wait_ge(const_done, 2 + 2 * QB)
            pe.wait_ge(count_done, 2)
            nc.tensor.matmul(denom[0:1, 0:1], count[:], ones[:, 0:1], start=True, stop=True).then_inc(total_done, 1)

            def scores(quad, m, j):
                buf, k = m // NROW % QB, m % NROW
                lt, h = k // G, k % G
                if k == 0 and j == 0:
                    pe.wait_ge(qk_in[buf], quad * 96 + 96 * (m // (NROW * QUAD) + 1))
                if not (isinstance(quad, int) and quad * QUAD * NROW + m == 0):
                    pe.wait_ge(max_done, quad * (2 * QUAD * NROW) + (2 * m + j - 1 + MAX0))
                s0, s1, w = HALVES[j]
                for c, start in enumerate((s0, s1)):
                    last = nc.tensor.matmul(score[j][:, c, 0:w], q_sb[buf][0:STACK, h, lt * P:(lt + 1) * P], k_sb[buf][0:STACK, start:start + w], start=True, stop=True)
                last.then_inc(score_done, 1)

            def turn(quad, s):
                step = quad * QUAD + s
                pe.wait_ge(rest_done, step * 4 + 4)
                if not (isinstance(step, int) and step == 0):
                    pe.wait_ge(exp_done, quad * (QUAD * ST * G) + (((s - 1) * ST + TURN_AT) * G + 3))
                pe.sem_inc(parts_seen, 1)
                nc.tensor.transpose(logit[0][0:3 * NROW, 0:P], parts[:].bitcast(F32).rearrange("p a r -> p (a r)"), ident[:]).then_inc(turn_done, 1)

            def logits(quad, s, st, h, masked):
                n = (s * ST + st) * G + h
                if st == 0 and h == 0:
                    pe.wait_ge(shift_in[s], quad * 48 + 48)
                    if masked:
                        pe.wait_ge(mask_exp_ready, quad + 1)
                if not (isinstance(quad, int) and quad == 0 and n < 2):
                    pe.wait_ge(exp_done, quad * (QUAD * ST * G) + (n - 1))
                if st == TURN_AT + 1 and h == 0:
                    step = quad * QUAD + s
                    pe.wait_ge(turn_copied, NSTEP if isinstance(step, int) and step == NSTEP - 1 else step + 2)
                w = min(P, S - st * P)
                keys = slice(st * P, st * P + w)
                bank = logit[h % 2]
                last = nc.tensor.matmul(bank[0:w, :], k_sb[s][:, keys], q_sb[s][:, h, :], start=True, stop=not masked, skip_group_check=masked)
                if masked:
                    for lt in range(NLT):
                        last = nc.tensor.matmul(bank[0:w, lt * P:(lt + 1) * P], mask_exp[:, lt, keys], ident[:], start=False, stop=(lt == NLT - 1), skip_group_check=True)
                last.then_inc(logit_done, 1)

            def sum_heads(out, lhs, rhs, w, start, stop, a=0, b=LQ):
                for h in range(G):
                    last = nc.tensor.matmul(out[h * HD:(h + 1) * HD, a:b], lhs, rhs[0:w, h, a:b], start=start, stop=stop, skip_group_check=b - a < LQ)
                return last

            def mix(quad, tile, a=0, b=LQ):
                s, st = tile // ST % QUAD, tile % ST
                if a == 0:
                    if st == 0:
                        pe.wait_ge(v_in[s], quad * 32 + 32)
                        if not (isinstance(quad, int) and quad * QUAD + s == 0):
                            pe.wait_ge(mixed_copied, quad * QUAD + s)
                    pe.wait_ge(exp_done, quad * (QUAD * ST * G) + (tile + 1) * G)
                w = min(P, S - st * P)
                last = sum_heads(mixed, v_sb[s][0:w, st, :], weights[buffer(s, st)], w, st == 0, st == ST - 1, a, b)
                if b == LQ:
                    last.then_inc(mix_done, 1)

            def total(quad, tile):
                s, st = tile // ST % QUAD, tile % ST
                if st == REST[0] and not (isinstance(quad, int) and quad * QUAD + s == 0):
                    pe.wait_ge(denom_copied, quad * QUAD + s)
                pe.wait_ge(exp_done, quad * (QUAD * ST * G) + (tile + 1) * G)
                w = min(P, S - st * P)
                sum_heads(denom, ones[0:w, :], weights[buffer(s, st)], w, st == REST[0], False)

            def denominators(step, par):
                pe.wait_ge(pool_added, step * NPOOL + NPOOL)
                sum_heads(denom, ones[:], sum_pool[par], P, False, True).then_inc(denom_done, 1)

            def quad_steps(quad, masked, first=False, last=False):
                for s in range(QUAD):
                    k = 0
                    for st in range(ST):
                        tile = s * ST + st
                        for h in range(G):
                            logits(quad, s, st, h, masked)
                            if h == 1:
                                if st == SUMS_AT and not (first and s == 0):
                                    denominators(quad * QUAD + (s - 1), (s - 1) % 2)
                                if (tile - LAG) % ST in REST and not (first and tile < LAG):
                                    total(quad, tile - LAG)
                            if h == 2 and DENSE[st] and not (first and tile < LAG):
                                mix(quad, tile - LAG)
                            if h == G - 1 and st == TURN_AT and not (last and s == QUAD - 1):
                                turn(quad, s + 1)
                            for _ in range(PACE[st][h]):
                                m = NROW * (s + 1) + LEAD + k // 2
                                if not (last and m >= QUAD * NROW):
                                    scores(quad, m, k % 2)
                                k += 1
                            if h % 2 and not DENSE[st] and not (first and tile < LAG):
                                mix(quad, tile - LAG, h // 2 * LQ // 2, (h // 2 + 1) * LQ // 2)

            def steps(masked):
                for m in range(NROW + LEAD):
                    for j in range(2):
                        scores(0, m, j)
                    if m == NROW + 1:
                        turn(0, 0)
                quad_steps(0, masked, first=True)
                with pe.Fori(1, NQUAD - 1) as quad:
                    quad_steps(quad, masked)
                quad_steps(NQUAD - 1, masked, last=True)
                for tile in range(QUAD * ST - LAG, QUAD * ST):
                    total(NQUAD - 1, tile)
                    mix(NQUAD - 1, tile)
                denominators(NSTEP - 1, 1)

            pe.wait_ge(flag_done, 1)
            any_mask = pe.value_load(flag[0:1, 0:1], min_val=0, max_val=1)
            with pe.If(any_mask > 0):
                steps(True)
            with pe.Else():
                steps(False)

        @block.vector
        def _(dve):
            dve.sem_inc(max_done, MAX0)
            nc.vector.tensor_reduce(count[:], mask_size[:], mybir.AxisListType.X, ALU.max).then_inc(count_done, 1)
            dve.wait_ge(count_done, 1)
            nc.vector.tensor_scalar(count[:], count[:], 0.0, None, ALU.not_equal).then_inc(count_done, 1)
            dve.wait_ge(total_done, 1)
            nc.vector.tensor_scalar(flag[:], denom[0:1, 0:1], 0.0, None, ALU.not_equal).then_inc(flag_done, 1)
            dve.wait_ge(const_done, 2 + 2 * QB)

            def maxima(quad, m, j):
                k = m % NROW
                lt, h = k // G, k % G
                n = quad * (2 * QUAD * NROW) + 2 * m
                if h == 0 and j == 0:
                    dve.wait_ge(mask_ready[lt], quad + (m // (QUAD * NROW) + 1))
                dve.wait_ge(score_done, n + (j + 1))
                if j:
                    dve.wait_ge(max_done, n + (1 + MAX0))
                dve.sem_inc(half_seen, 1)
                s0, _, w = HALVES[j]
                half, whole = half_max[:, m % 2:m % 2 + 1], row_max[m // NROW % 2][:, h, lt:lt + 1]
                nc.vector.tensor_tensor_reduce(
                    masked_row[j][:].rearrange("p (c s) -> p c s", c=2), score[j][:, :, 0:w],
                    mask_max[:, lt, s0:s0 + 2 * w].rearrange("p (c s) -> p c s", c=2), 1.0,
                    half if j else -FMAX, ALU.add, ALU.max, whole if j else half).then_inc(max_done, 1)

            def split(step, par):
                top = row_max[par][:].rearrange("p h t -> p (h t)")
                dve.wait_ge(max_done, step * (2 * NROW) + (2 * NROW + MAX0))
                if not (isinstance(step, int) and step == 0):
                    dve.wait_ge(turn_done, step)
                nc.vector.tensor_scalar(parts[:, 0, :], top, -1.0, None, ALU.mult).then_inc(rest_done, 1)
                dve.wait_ge(rest_done, step * 4 + 1)
                nc.vector.scalar_tensor_tensor(out=rest[:], in0=top, scalar=-1.0, in1=parts[:, 0, :].bitcast(F32), op0=ALU.mult, op1=ALU.subtract).then_inc(rest_done, 1)
                dve.wait_ge(rest_done, step * 4 + 2)
                nc.vector.tensor_scalar(parts[:, 1, :], rest[:], 1.0, None, ALU.mult).then_inc(rest_done, 1)
                dve.wait_ge(rest_done, step * 4 + 3)
                nc.vector.tensor_tensor(parts[:, 2, :], rest[:], parts[:, 1, :].bitcast(F32), ALU.subtract).then_inc(rest_done, 1)

            def quad_steps(quad, first=False, last=False):
                for s in range(QUAD):
                    for k in range(2 * NROW):
                        m = NROW * (s + 1) + LEAD + k // 2
                        if not (last and m >= QUAD * NROW):
                            maxima(quad, m, k % 2)
                        if k == 2 * (NROW - LEAD) - 1 and not (last and s == QUAD - 1):
                            split(quad * QUAD + (s + 1), (s + 1) % 2)

            for m in range(NROW + LEAD):
                for j in range(2):
                    maxima(0, m, j)
                if m == NROW - 1:
                    split(0, 0)
            quad_steps(0, first=True)
            with dve.Fori(1, NQUAD - 1) as quad:
                quad_steps(quad)
            quad_steps(NQUAD - 1, last=True)

        @block.scalar
        def _(act):
            for i in range(2):
                act.sem_inc(mixed_stored[i], 16)
                act.sem_inc(denom_stored[i], 16)

            def exponents(quad, s, st, h):
                n = (s * ST + st) * G + h
                before, old = tile_before(s, st)
                if h == 0 and not (isinstance(quad, int) and quad == 0 and before < 0):
                    act.wait_ge(mix_done, quad * (QUAD * ST) + (before * ST + old + 1 + MIX0))
                    if old in POOL:
                        act.wait_ge(pool_added, quad * (QUAD * NPOOL) + (before * NPOOL + max(POOL.index(old), 1)))
                act.wait_ge(logit_done, quad * (QUAD * ST * G) + (n + 1 + LOGITS0))
                w = min(P, S - st * P)
                nc.scalar.activation(weights[buffer(s, st)][0:w, h, :], logit[h % 2][0:w, :], ACT.Exp).then_inc(exp_done, 1)

            def copy_parts(step, before, uses):
                act.wait_ge(turn_done, step + 1)
                if before is not None:
                    act.wait_ge(shift_in[before], uses)
                nc.scalar.copy(parts_t[:], logit[0][0:3 * NROW, 0:P]).then_inc(turn_copied, 1)

            def copy_mixed(quad, s):
                act.wait_ge(mix_done, quad * (QUAD * ST) + ((s + 1) * ST + MIX0))
                act.wait_ge(mixed_stored[s % 2], quad * 32 + (16 * (s // 2) + 16))
                nc.scalar.copy(mixed_sb[s % 2][:], mixed[:]).then_inc(mixed_copied, 1)

            def copy_denominators(quad, s):
                act.wait_ge(denom_done, quad * QUAD + (s + 3))
                act.wait_ge(denom_stored[s % 2], quad * 32 + (16 * (s // 2) + 16))
                nc.scalar.copy(denom_sb[s % 2][:], denom[:]).then_inc(denom_copied, 1)

            def quad_steps(quad, first=False, last=False):
                for s in range(QUAD):
                    for st in range(ST):
                        for h in range(G):
                            exponents(quad, s, st, h)
                            if h == 0 and not (first and s == 0):
                                if st == MIXED_AT:
                                    copy_mixed(quad, s - 1)
                                if st == DENOM_AT:
                                    copy_denominators(quad, s - 1)
                        if st == TURN_AT and not (last and s == QUAD - 1):
                            copy_parts(quad * QUAD + (s + 1), s, quad * 48 + 48)

            copy_parts(0, None, 0)
            quad_steps(0, first=True)
            with act.Fori(1, NQUAD - 1) as quad:
                quad_steps(quad)
            quad_steps(NQUAD - 1, last=True)
            copy_mixed(NQUAD - 1, QUAD - 1)
            copy_denominators(NQUAD - 1, QUAD - 1)


def output(nc, x_flat, wo, wo_early, bo, gamma, beta, a_dram, d_dram, r_dram, out_flat):
    NT = OQ // P
    NOB = B * L // OQ
    with ExitStack() as held:
        def sb(name, shape, dt=F32):
            return held.enter_context(nc.sbuf_tensor(name, shape, dt))

        def sem(name):
            return held.enter_context(nc.semaphore(name))

        wo_late = sb("wo_late", [P, KVH - EARLY, H])
        wo_hi, wo_lo = sb("wo_hi", [P, KVH, H], F32R), sb("wo_lo", [P, KVH, H], F32R)
        bo_row, gamma_row, beta_row = sb("bo_row", [P, H]), sb("gamma_row", [P, H]), sb("beta_row", [P, H])
        a_in = [sb(f"a_in{i}", [P, KVH, OQ]) for i in range(2)]
        r_in = [sb(f"r_in{i}", [P, KVH, OQ]) for i in range(2)]
        dens = [sb(f"dens{i}", [P, steps * G * LQ // P]) for i, steps in enumerate((KVH, NSTEP - KVH))]
        a_hi = [sb(f"a_hi{i}", [P, KVH, OQ], F32R) for i in range(2)]
        a_lo = [sb(f"a_lo{i}", [P, KVH, OQ], F32R) for i in range(2)]
        resid = [sb(f"resid{i}", [P, H]) for i in range(NT)]
        total = [sb(f"total{i}", [P, H]) for i in range(NT)]
        stats = [sb(f"stats{i}", [P, 2, 6]) for i in range(NT)]
        moments = [sb(f"moments{i}", [P, 2]) for i in range(NT)]
        spread = [sb(f"spread{i}", [P, 2]) for i in range(NT)]
        eps = sb("eps", [P, 1])
        acc = [held.enter_context(nc.psum_tensor(f"acc{i}", [P, 2, 512], F32)) for i in range(NT)]

        rows_in = sem("rows_const_in")
        w_in = [sem(f"wo_in{k}") for k in range(EARLY, KVH)]
        w_hi_done, w_lo_done = sem("wo_hi_done"), sem("wo_lo_done")
        eps_done = sem("eps_done")
        dens_in, dens_recip, dens_out = [sem(f"dens_in{i}") for i in range(2)], sem("dens_recip"), [sem(f"dens_out{i}") for i in range(2)]
        a_landed = [sem(f"a_landed{i}") for i in range(2)]
        normed_done = sem("normed_done")
        a_hi_done, a_lo_done = sem("a_hi_done"), sem("a_lo_done")
        x_landed = [sem(f"x_landed{i}") for i in range(NT)]
        resid_done = sem("resid_done")
        proj_done = sem("proj_done")
        total_done = sem("total_done")
        chain = sem("chain")
        stats_seen = sem("stats_seen")
        std_done = sem("std_done")
        recip_done = sem("std_recip_done")
        scaled = sem("scaled")
        final = sem("final")
        stored = sem("out_stored")
        free = [sem(f"total_free{i}") for i in range(NT)]

        def raw(k):
            return wo_early[:, k, :] if k < EARLY else wo_late[:, k - EARLY, :]

        block = held.enter_context(nc.Block())

        @block.sync
        def _(sp):
            def portion(dram, n):
                steps = dram[0:KVH] if n == 0 else dram[KVH:NSTEP]
                return steps.rearrange("a h l -> (a h l)").rearrange("(p n) -> p n", p=P)

            def store_reciprocals(n):
                sp.wait_ge(dens_recip, n + 1)
                sp.dma_start(portion(r_dram, n), dens[n][:]).then_inc(dens_out[n], 16)
                sp.wait_ge(dens_out[n], 16)

            for n in range(2):
                sp.dma_start(dens[n][:], portion(d_dram, n)).then_inc(dens_in[n], 16)

            def load_block(i, j):
                sp.wait_ge(a_lo_done, i * 2 + (j + 1))
                cols = slice(j * OQ, (j + 1) * OQ)
                sp.dma_start(a_in[j][:], a_dram[bass.ds(i * KVH, KVH), :, cols].rearrange("k p l -> p k l")).then_inc(a_landed[j], 16)
                for h in range(G):
                    sp.dma_start(r_in[j][h * HD:(h + 1) * HD], r_dram[bass.ds(i * KVH, KVH), h, cols].partition_broadcast(HD)).then_inc(a_landed[j], 16)

            def load_x(i, j):
                for t in range(NT):
                    sp.wait_ge(total_done, i * (2 * NT) + (j * NT + t + 1))
                    sp.dma_start(resid[t][:], x_flat[bass.ds(i * (2 * OQ) + (j * OQ + t * P), P), :]).then_inc(x_landed[t], 16)

            store_reciprocals(0)
            for j in range(2):
                load_block(0, j)
            store_reciprocals(1)
            for row, src in ((bo_row, bo), (gamma_row, gamma), (beta_row, beta)):
                sp.dma_start(row[:], src.partition_broadcast(P)).then_inc(rows_in, 16)
            with sp.Fori(0, NOB // 2 - 1) as i:
                for j in range(2):
                    load_x(i, j)
                    load_block(i + 1, j)
            for j in range(2):
                load_x(NOB // 2 - 1, j)

        @block.tensor
        def _(pe):
            pe.sem_inc(proj_done, 2 * NT)
            with pe.Fori(0, NOB // 2) as i:
                for j in range(2):
                    pe.wait_ge(a_lo_done, i * 2 + (j + 3))
                    for t in range(NT):
                        pe.wait_ge(total_done, i * (2 * NT) + (j * NT + t + 1))
                        cols = slice(t * P, (t + 1) * P)
                        for n in range(2):
                            out_cols = slice(n * 512, (n + 1) * 512)
                            for k in range(KVH):
                                if t == 0 and n == 0:
                                    pe.wait_ge(w_lo_done, k + 1)
                                for m, (a, w) in enumerate(((a_hi[j], wo_hi), (a_lo[j], wo_hi), (a_hi[j], wo_lo))):
                                    last = nc.tensor.matmul(acc[t][:, n, :], a[:, k, cols], w[:, k, out_cols], start=(k == 0 and m == 0), stop=(k == KVH - 1 and m == 2))
                        last.then_inc(proj_done, 1)

        @block.scalar
        def _(act):
            def split_weights(slices):
                for k in slices:
                    if k >= EARLY:
                        act.wait_ge(w_in[k - EARLY], 16)
                    nc.scalar.copy(wo_hi[:, k, :], raw(k)).then_inc(w_hi_done, 1)

            for k in range(EARLY, KVH):
                act.dma_start(raw(k), wo[k * P:(k + 1) * P, :]).then_inc(w_in[k - EARLY], 16)

            def split_hi(pair, j):
                act.wait_ge(normed_done, pair * 2 + (j + 1))
                act.wait_ge(proj_done, (pair * 2 + j) * NT + NT)
                nc.scalar.copy(a_hi[j][:], a_in[j][:]).then_inc(a_hi_done, 1)

            def deviations(pair, j):
                for t in range(NT):
                    act.wait_ge(chain, ((pair * 2 + j) * NT + (t + 1)) * 3)
                    nc.scalar.activation(spread[t][:, 0:1], moments[t][:, 1:2], ACT.Sqrt, bias=eps[:]).then_inc(std_done, 1)

            split_weights(range(KVH // 2))
            split_hi(0, 0)
            split_weights(range(KVH // 2, KVH))
            act.wait_ge(eps_done, 1)
            with act.Fori(0, NOB // 2 - 1) as i:
                split_hi(i, 1)
                deviations(i, 0)
                split_hi(i + 1, 0)
                deviations(i, 1)
            split_hi(NOB // 2 - 1, 1)
            deviations(NOB // 2 - 1, 0)
            deviations(NOB // 2 - 1, 1)

        @block.vector
        def _(dve):
            dve.sem_inc(a_lo_done, 2)
            dve.sem_inc(total_done, NT)
            for n in range(2):
                dve.wait_ge(dens_in[n], 16)
                nc.vector.reciprocal(dens[n][:], dens[n][:]).then_inc(dens_recip, 1)

            def split_weights(slices):
                for k in slices:
                    dve.wait_ge(w_hi_done, k + 1)
                    nc.vector.tensor_tensor(wo_lo[:, k, :], raw(k), wo_hi[:, k, :].bitcast(F32), ALU.subtract).then_inc(w_lo_done, 1)

            def normalise(i, j):
                dve.wait_ge(a_landed[j], i * (16 + 16 * G) + (16 + 16 * G))
                nc.vector.tensor_tensor(a_in[j][:], a_in[j][:], r_in[j][:], ALU.mult).then_inc(normed_done, 1)

            def split_lo(i, j):
                dve.wait_ge(a_hi_done, i * 2 + (j + 1))
                nc.vector.tensor_tensor(a_lo[j][:], a_in[j][:], a_hi[j][:].bitcast(F32), ALU.subtract).then_inc(a_lo_done, 1)

            def norm(i, j):
                for t in range(NT):
                    n = i * (2 * NT) + (j * NT + t)
                    dve.wait_ge(proj_done, n + (2 * NT + 1))
                    dve.wait_ge(resid_done, n + 1)
                    dve.wait_ge(free[t], i * 2 + (j + 1))
                    nc.vector.tensor_tensor(total[t][:].rearrange("p (c n) -> p c n", c=2), acc[t][:], resid[t][:].rearrange("p (c n) -> p c n", c=2), ALU.add).then_inc(total_done, 1)
                    dve.wait_ge(total_done, n + (NT + 1))
                    for c in range(2):
                        nc.vector.bn_stats(stats[t][:, c, :], total[t][:, c * 512:(c + 1) * 512]).then_inc(chain, 1)
                    dve.wait_ge(chain, n * 3 + 2)
                    dve.sem_inc(stats_seen, 1)
                    nc.vector.bn_aggr(moments[t][:], stats[t][:].rearrange("p c s -> p (c s)")).then_inc(chain, 1)
                    dve.wait_ge(std_done, n + 1)
                    nc.vector.reciprocal(spread[t][:, 1:2], spread[t][:, 0:1]).then_inc(recip_done, 1)
                    dve.wait_ge(recip_done, n + 1)
                    nc.vector.tensor_scalar(total[t][:], total[t][:], moments[t][:, 0:1], spread[t][:, 1:2], ALU.subtract, ALU.mult).then_inc(scaled, 1)
                    dve.wait_ge(scaled, n * 2 + 1)
                    nc.vector.tensor_tensor(total[t][:], total[t][:], gamma_row[:], ALU.mult).then_inc(scaled, 1)

            split_weights(range(KVH // 2))
            normalise(0, 0)
            split_lo(0, 0)
            split_weights(range(KVH // 2, KVH))
            normalise(0, 1)
            with dve.Fori(0, NOB // 2 - 1) as i:
                split_lo(i, 1)
                normalise(i + 1, 0)
                norm(i, 0)
                split_lo(i + 1, 0)
                normalise(i + 1, 1)
                norm(i, 1)
            split_lo(NOB // 2 - 1, 1)
            norm(NOB // 2 - 1, 0)
            norm(NOB // 2 - 1, 1)

        @block.gpsimd
        def _(pool):
            nc.gpsimd.memset(eps[:], EPS).then_inc(eps_done, 1)
            for t in range(NT):
                pool.sem_inc(free[t], 1)
            pool.wait_ge(rows_in, 48)

            def add_bias(i, j, t):
                pool.wait_ge(x_landed[t], i * 32 + (j * 16 + 16))
                nc.gpsimd.tensor_tensor(resid[t][:], resid[t][:], bo_row[:], ALU.add).then_inc(resid_done, 1)

            with pool.Fori(0, NOB // 2) as i:
                for j in range(2):
                    for t in range(NT):
                        add_bias(i, j, t)
                    for t in range(NT):
                        n = i * (2 * NT) + (j * NT + t)
                        pool.wait_ge(scaled, n * 2 + 2)
                        nc.gpsimd.tensor_tensor(total[t][:], total[t][:], beta_row[:], ALU.add).then_inc(final, 1)
                        pool.wait_ge(final, n + 1)
                        pool.dma_start(out_flat[bass.ds(i * (2 * OQ) + (j * OQ + t * P), P), :], total[t][:]).then_inc(stored, 16)
                        pool.wait_ge(stored, n * 16 + 16)
                        pool.sem_inc(free[t], 1)


_INS = ["x", "ctx_2048", "mask_Bx1xSxS2_ff0"] + ["L0_xattn_" + n for n in ("Wq", "bq", "Wk", "bk", "Wv", "bv", "Wo", "bo", "gamma", "beta")]


def kernel(**inputs):
    import concourse.bacc as bacc
    from concourse.bass_utils import run_bass_kernel_spmd

    nc = bacc.Bacc("TRN2", target_bir_lowering=False, num_devices=1)
    arrays, args = {}, []
    for name in _INS:
        a = np.ascontiguousarray(inputs[name])
        arrays[f"in_{name}"] = a
        args.append(nc.dram_tensor(f"in_{name}", a.shape, mybir.dt.from_np(a.dtype), kind="ExternalInput").ap())
    out = nc.dram_tensor("out", (B, L, H), F32, kind="ExternalOutput").ap()
    xattn_program(nc, *args, out)
    r = run_bass_kernel_spmd(nc, [arrays], core_ids=[0])
    return r.results[0]["out"]
```
